# Optimizing a Trainium2 kernel written in Bass

```python
import numpy as np
import jax
import jax.numpy as jnp

def _softmax(x, axis=-1):
    return jax.nn.softmax(x, axis=axis)

def _gelu(x):
    return jax.nn.gelu(x, approximate=True)

def _silu(x):
    return jax.nn.silu(x)

def _sigmoid(x):
    return jax.nn.sigmoid(x)

def _layernorm(x, axis=-1, eps=1e-05):
    m = jnp.mean(x, axis=axis, keepdims=True)
    v = jnp.var(x, axis=axis, keepdims=True)
    return (x - m) / jnp.sqrt(v + eps)

def _scatter_add(tgt, idx, src, axis=0):
    return tgt.at[idx].add(src)

def _segment_sum(src, seg, n):
    return jax.ops.segment_sum(src, seg, n)
kernel_name = 'mk_gnn_resnorm_d4_gnn_r8_09395f'

def setup_inputs(seed: int=0):
    np.random.seed(seed)
    _w = jnp.asarray

    def _rec_inputs():
        import jax
        import jax.numpy as jnp
        _gk = jax.random.key(seed)
        x = -0.0003713 + 1 * jax.random.normal(jax.random.fold_in(_gk, 1), (6250, 128), jnp.float32)
        _s = jax.random.randint(jax.random.fold_in(_gk, 2), (50000,), 0, 6250, jnp.int32)
        _d = jax.random.randint(jax.random.fold_in(_gk, 3), (50000,), 0, 6250, jnp.int32)
        _loop = jnp.arange(6250, dtype=jnp.int32)
        src = jnp.concatenate([_s, _d, _loop])
        dst = jnp.concatenate([_d, _s, _loop])
        _o = jnp.argsort(dst, stable=True)
        src = src[_o]
        dst = dst[_o]
        edge_attr_32 = -9.77346e-05 + 0.999888 * jax.random.normal(jax.random.fold_in(_gk, 11), (106250, 32), jnp.float32)
        edge_weight = jax.random.uniform(jax.random.fold_in(_gk, 13), (106250,), jnp.float32, 0.0, 0.999998)
        return (x, src, dst, edge_attr_32, edge_weight)
    x, src, dst, edge_attr_32, edge_weight = _rec_inputs()

    def _L0_gnn_setup():
        import jax, jax.numpy as jnp
        import numpy as np
        N_NODES = 12500
        N_EDGES = 200000
        D = 128
        K = 2
        ALPHA = 0.5

        def _appnp(x, edge_index):
            n = x.shape[0]
            loops = jnp.arange(n, dtype=edge_index.dtype)
            src = jnp.concatenate([edge_index[0], loops])
            dst = jnp.concatenate([edge_index[1], loops])
            ew = jnp.ones_like(src, dtype=x.dtype)
            deg = jax.ops.segment_sum(ew, dst, num_segments=n)
            dinv = jnp.where(deg > 0, jax.lax.rsqrt(deg), 0.0)
            norm = dinv[src] * ew * dinv[dst]
            h = x
            for _ in range(K):
                msg = norm[:, None] * x[src]
                agg = jax.ops.segment_sum(msg, dst, num_segments=n)
                x = (1.0 - ALPHA) * agg + ALPHA * h
            return x
        key = jax.random.key(seed)
        ks = jax.random.split(key, 5)
        x = jax.random.normal(ks[0], (N_NODES, D), dtype=jnp.float32)
        edge_index = jax.random.randint(ks[1], (2, N_EDGES), 0, N_NODES, dtype=jnp.int32)
        s = 1.0 / np.sqrt(D)
        w1 = jax.random.uniform(ks[2], (D, D), jnp.float32, -s, s)
        b1 = jnp.zeros((D,), jnp.float32)
        w2 = jax.random.uniform(ks[3], (D, D), jnp.float32, -s, s)
        b2 = jnp.zeros((D,), jnp.float32)
        return {'x': x, 'edge_index': edge_index, 'w1': w1, 'b1': b1, 'w2': w2, 'b2': b2}
    _L0_gnn_all = _L0_gnn_setup()
    _L0_gnn_in = {k: v for k, v in _L0_gnn_all.items() if k in ('w1', 'b1', 'w2', 'b2')}
    del _L0_gnn_all

    def _L1_gnn_setup():
        import jax, jax.numpy as jnp
        import numpy as np
        N = 12500
        E = 200000
        IN_CH = 128
        HEADS = 4
        OUT_CH = 32
        NEG_SLOPE = 0.2
        key = jax.random.key(seed)
        k1, k2, k3, k4 = jax.random.split(key, 4)
        x = jax.random.normal(k1, (N, IN_CH), dtype=jnp.float32)
        edge_index = jax.random.randint(k2, (2, E), 0, N, dtype=jnp.int64)
        w_lim = float(np.sqrt(6.0 / (IN_CH + HEADS * OUT_CH)))
        a_lim = float(np.sqrt(6.0 / (HEADS + 2 * OUT_CH)))
        weight = jax.random.uniform(k3, (IN_CH, HEADS * OUT_CH), dtype=jnp.float32, minval=-w_lim, maxval=w_lim)
        att = jax.random.uniform(k4, (1, HEADS, 2 * OUT_CH), dtype=jnp.float32, minval=-a_lim, maxval=a_lim)
        bias = jnp.zeros((HEADS * OUT_CH,), dtype=jnp.float32)
        return {'x': x, 'edge_index': edge_index, 'weight': weight, 'att': att, 'bias': bias}
    _L1_gnn_all = _L1_gnn_setup()
    _L1_gnn_in = {k: v for k, v in _L1_gnn_all.items() if k in ('weight', 'att', 'bias')}
    del _L1_gnn_all

    def _L2_gnn_setup():
        import jax, jax.numpy as jnp
        import numpy as np
        N_NODES = 12500
        N_EDGES = 125000
        EMB_DIM = 128
        NEG_SLOPE = 0.01
        key = jax.random.key(seed)
        k1, k2, k3, k4 = jax.random.split(key, 4)
        x = jax.random.normal(k1, (N_NODES, EMB_DIM), dtype=jnp.float32)
        edge_index = jax.random.randint(k2, (2, N_EDGES), 0, N_NODES, dtype=jnp.int64)
        edge_attrs = jax.random.uniform(k3, (N_EDGES,), dtype=jnp.float32)
        limit = float(np.sqrt(6.0 / (EMB_DIM + EMB_DIM)))
        W1_w = jax.random.uniform(k4, (EMB_DIM, EMB_DIM), dtype=jnp.float32, minval=-limit, maxval=limit)
        W1_b = jnp.zeros((EMB_DIM,), dtype=jnp.float32)
        return {'x': x, 'edge_index': edge_index, 'edge_attrs': edge_attrs, 'W1_w': W1_w, 'W1_b': W1_b}
    _L2_gnn_all = _L2_gnn_setup()
    _L2_gnn_in = {k: v for k, v in _L2_gnn_all.items() if k in ('W1_w', 'W1_b')}
    del _L2_gnn_all

    def _L3_gnn_setup():
        import jax, jax.numpy as jnp
        import numpy as np
        N_NODES = 6250
        N_EDGES = 200000
        IN_DIM = 128
        OUT_DIM = 32
        HEADS = 4
        EDGE_DIM = 32
        HD = HEADS * OUT_DIM
        key = jax.random.key(seed)
        ks = jax.random.split(key, 12)
        s_in = 1.0 / np.sqrt(IN_DIM)
        s_e = 1.0 / np.sqrt(EDGE_DIM)
        return {'x': jax.random.normal(ks[0], (N_NODES, IN_DIM), jnp.float32), 'edge_attr': jax.random.normal(ks[1], (N_EDGES, EDGE_DIM), jnp.float32), 'edge_index': jax.random.randint(ks[2], (2, N_EDGES), 0, N_NODES, jnp.int32), 'Wq': jax.random.normal(ks[3], (IN_DIM, HD), jnp.float32) * s_in, 'bq': jnp.zeros((HD,), jnp.float32), 'Wk': jax.random.normal(ks[4], (IN_DIM, HD), jnp.float32) * s_in, 'bk': jnp.zeros((HD,), jnp.float32), 'Wv': jax.random.normal(ks[5], (IN_DIM, HD), jnp.float32) * s_in, 'bv': jnp.zeros((HD,), jnp.float32), 'We': jax.random.normal(ks[6], (EDGE_DIM, HD), jnp.float32) * s_e, 'Wskip': jax.random.normal(ks[7], (IN_DIM, HD), jnp.float32) * s_in, 'bskip': jnp.zeros((HD,), jnp.float32)}
    _L3_gnn_all = _L3_gnn_setup()
    _L3_gnn_in = {k: v for k, v in _L3_gnn_all.items() if k in ('Wq', 'bq', 'Wk', 'bk', 'Wv', 'bv', 'We', 'Wskip', 'bskip')}
    del _L3_gnn_all
    return {'x': x, 'src': src, 'dst': dst, 'edge_attr_32': edge_attr_32, 'edge_weight': edge_weight, 'L0_gnn_w1': _L0_gnn_in['w1'], 'L0_gnn_b1': _L0_gnn_in['b1'], 'L0_gnn_w2': _L0_gnn_in['w2'], 'L0_gnn_b2': _L0_gnn_in['b2'], 'L1_gnn_weight': _L1_gnn_in['weight'], 'L1_gnn_att': _L1_gnn_in['att'], 'L1_gnn_bias': _L1_gnn_in['bias'], 'L2_gnn_W1_w': _L2_gnn_in['W1_w'], 'L2_gnn_W1_b': _L2_gnn_in['W1_b'], 'L3_gnn_Wq': _L3_gnn_in['Wq'], 'L3_gnn_bq': _L3_gnn_in['bq'], 'L3_gnn_Wk': _L3_gnn_in['Wk'], 'L3_gnn_bk': _L3_gnn_in['bk'], 'L3_gnn_Wv': _L3_gnn_in['Wv'], 'L3_gnn_bv': _L3_gnn_in['bv'], 'L3_gnn_We': _L3_gnn_in['We'], 'L3_gnn_Wskip': _L3_gnn_in['Wskip'], 'L3_gnn_bskip': _L3_gnn_in['bskip']}

def reference(x, src, dst, edge_attr_32, edge_weight, L0_gnn_w1, L0_gnn_b1, L0_gnn_w2, L0_gnn_b2, L1_gnn_weight, L1_gnn_att, L1_gnn_bias, L2_gnn_W1_w, L2_gnn_W1_b, L3_gnn_Wq, L3_gnn_bq, L3_gnn_Wk, L3_gnn_bk, L3_gnn_Wv, L3_gnn_bv, L3_gnn_We, L3_gnn_Wskip, L3_gnn_bskip):
    import jax
    import jax.numpy as jnp

    def _L0_gnn_ref(x, edge_index, w1, b1, w2, b2):
        import jax, jax.numpy as jnp
        import numpy as np
        N_NODES = 12500
        N_EDGES = 200000
        D = 128
        K = 2
        ALPHA = 0.5

        def _appnp(x, edge_index):
            n = x.shape[0]
            loops = jnp.arange(n, dtype=edge_index.dtype)
            src = jnp.concatenate([edge_index[0], loops])
            dst = jnp.concatenate([edge_index[1], loops])
            ew = jnp.ones_like(src, dtype=x.dtype)
            deg = jax.ops.segment_sum(ew, dst, num_segments=n)
            dinv = jnp.where(deg > 0, jax.lax.rsqrt(deg), 0.0)
            norm = dinv[src] * ew * dinv[dst]
            h = x
            for _ in range(K):
                msg = norm[:, None] * x[src]
                agg = jax.ops.segment_sum(msg, dst, num_segments=n)
                x = (1.0 - ALPHA) * agg + ALPHA * h
            return x
        x = jax.nn.relu(_appnp(x, edge_index))
        x = x @ w1.T + b1
        x = x @ w2.T + b2
        return x

    def _L1_gnn_ref(x, edge_index, weight, att, bias):
        import jax, jax.numpy as jnp
        import numpy as np
        N = 12500
        E = 200000
        IN_CH = 128
        HEADS = 4
        OUT_CH = 32
        NEG_SLOPE = 0.2
        n = x.shape[0]
        h = jnp.matmul(x, weight).reshape(n, HEADS, OUT_CH)
        src, dst = (edge_index[0], edge_index[1])
        x_src = h[src]
        x_dst = h[dst]
        att_src = att[:, :, :OUT_CH]
        att_dst = att[:, :, OUT_CH:]
        alpha = (x_src * att_src).sum(-1) + (x_dst * att_dst).sum(-1)
        alpha = jnp.where(alpha >= 0, alpha, NEG_SLOPE * alpha)
        seg_max = jax.ops.segment_max(alpha, dst, num_segments=n)
        alpha = jnp.exp(alpha - seg_max[dst])
        seg_sum = jax.ops.segment_sum(alpha, dst, num_segments=n)
        alpha = alpha / (seg_sum[dst] + 1e-16)
        out = jax.ops.segment_sum(alpha[:, :, None] * x_src, dst, num_segments=n)
        out = out.reshape(n, HEADS * OUT_CH)
        return out + bias

    def _L2_gnn_ref(x, edge_index, edge_attrs, W1_w, W1_b):
        import jax, jax.numpy as jnp
        import numpy as np
        N_NODES = 12500
        N_EDGES = 125000
        EMB_DIM = 128
        NEG_SLOPE = 0.01
        n = x.shape[0]
        from_, to_ = (edge_index[0], edge_index[1])
        deg = jax.ops.segment_sum(jnp.ones((to_.shape[0],), dtype=x.dtype), to_, num_segments=n)
        deg_inv = jnp.where(deg > 0, 1.0 / jnp.sqrt(deg), 0.0)
        norm = deg_inv[from_] * deg_inv[to_]
        x_i = x[from_]
        x_j = x[to_]
        m_j = norm[:, None] * (x_j + x_j * x_i @ W1_w.T + W1_b)
        out = jax.ops.segment_sum(m_j, to_, num_segments=n)
        out = jnp.where(out >= 0, out, NEG_SLOPE * out)
        return out

    def _L3_gnn_ref(x, edge_attr, edge_index, Wq, bq, Wk, bk, Wv, bv, We, Wskip, bskip):
        import jax, jax.numpy as jnp
        import numpy as np
        N_NODES = 6250
        N_EDGES = 200000
        IN_DIM = 128
        OUT_DIM = 32
        HEADS = 4
        EDGE_DIM = 32
        HD = HEADS * OUT_DIM
        N = x.shape[0]
        src, dst = (edge_index[0], edge_index[1])
        scale = 1.0 / jnp.sqrt(jnp.asarray(OUT_DIM, x.dtype))
        q = (x @ Wq + bq).reshape(N, HEADS, OUT_DIM)
        k = (x @ Wk + bk).reshape(N, HEADS, OUT_DIM)
        v = (x @ Wv + bv).reshape(N, HEADS, OUT_DIM)
        e = (edge_attr @ We).reshape(-1, HEADS, OUT_DIM)
        k_j = k[src] + e
        v_j = v[src] + e
        logits = jnp.einsum('ehd,ehd->eh', q[dst], k_j) * scale
        m = jax.ops.segment_max(logits, dst, num_segments=N)
        m = jnp.where(jnp.isfinite(m), m, 0.0)
        p = jnp.exp(logits - m[dst])
        s = jax.ops.segment_sum(p, dst, num_segments=N)
        alpha = p / jnp.maximum(s[dst], 1e-16)
        msg = jax.ops.segment_sum(alpha[..., None] * v_j, dst, num_segments=N)
        out = msg.reshape(N, HD) + x @ Wskip + bskip
        return jax.nn.relu(out)
    edge_index = jnp.stack([src, dst])
    x = _layernorm(x + _L0_gnn_ref(x, edge_index, L0_gnn_w1, L0_gnn_b1, L0_gnn_w2, L0_gnn_b2), axis=-1)
    x = _layernorm(x + _L1_gnn_ref(x, edge_index, L1_gnn_weight, L1_gnn_att, L1_gnn_bias), axis=-1)
    x = _layernorm(x + _L2_gnn_ref(x, edge_index, edge_weight, L2_gnn_W1_w, L2_gnn_W1_b), axis=-1)
    x = _layernorm(x + _L3_gnn_ref(x, edge_attr_32, edge_index, L3_gnn_Wq, L3_gnn_bq, L3_gnn_Wk, L3_gnn_bk, L3_gnn_Wv, L3_gnn_bv, L3_gnn_We, L3_gnn_Wskip, L3_gnn_bskip), axis=-1)
    return x

_drawn_inputs = setup_inputs


def setup_inputs(seed=0):
    import zlib

    import numpy as np

    out = dict(_drawn_inputs(seed))
    spreads = {'L0_gnn_b1': (0.0, 0.1),
     'L0_gnn_b2': (0.0, 0.1),
     'L1_gnn_bias': (0.0, 0.1),
     'L2_gnn_W1_b': (0.0, 0.1),
     'L3_gnn_bq': (0.0, 0.1),
     'L3_gnn_bk': (0.0, 0.1),
     'L3_gnn_bv': (0.0, 0.1),
     'L3_gnn_bskip': (0.0, 0.1)}
    factors = {}
    for name, (base, spread) in spreads.items():
        noise = np.random.default_rng([zlib.crc32(name.encode()), seed]).standard_normal(out[name].shape)
        drawn = base * np.exp(spread * noise) if base else spread * noise
        out[name] = jnp.asarray(drawn.astype(out[name].dtype))
    for name, factor in factors.items():
        out[name] = (out[name] * factor).astype(out[name].dtype)
    return out
```

```python
from contextlib import ExitStack

import numpy as np
import concourse.bass as bass
import concourse.mybir as mybir

F32 = mybir.dt.float32
BF16 = mybir.dt.bfloat16
I32 = mybir.dt.int32
ALU = mybir.AluOpType
ACT = mybir.ActivationFunctionType
AX_X = mybir.AxisListType.X

P = 128
N_NODES = 6250
N_EDGES = 106250
D = 128
HEADS = 4
HC = D // HEADS
EDGE_DIM = 32

CHUNK = P
GROUP = 8
CHUNKS = -(-N_EDGES // (CHUNK * GROUP)) * GROUP
GROUPS = CHUNKS // GROUP
E_PAD = CHUNKS * CHUNK
RING = 4
ROUNDS = GROUPS // RING
HALF = GROUP // 2
TILES = 52
N_PAD = TILES * P
QUAD = 4
QUADS = TILES // QUAD
FULL_TILES, TAIL = divmod(N_NODES, P)
EPS = 1e-5
SUPERS = 8
ROWS = CHUNKS // SUPERS
SUPER_GROUPS = ROWS // GROUP
BIG = 1e30
assert ROWS * SUPERS == CHUNKS and SUPER_GROUPS * GROUP == ROWS
assert CHUNKS == ROUNDS * RING * GROUP and TILES == QUADS * QUAD


class Core:

    def __init__(self, nc):
        self.nc = nc

    def sb(self, ctx, name, shape, dt=F32):
        return ctx.enter_context(self.nc.sbuf_tensor(name, shape, dt))

    def ps(self, ctx, name, shape):
        return ctx.enter_context(self.nc.psum_tensor(name, shape, F32))

    def sem(self, name):
        return self.nc.alloc_semaphore(name)


def wide(ap, n):
    return ap.unsqueeze(2).to_broadcast([ap.shape[0], ap.shape[1], n])


def along(ap, k):
    return ap.unsqueeze(1).to_broadcast([ap.shape[0], k, ap.shape[1]])


def load_bases(eng, regs, base_row, first):
    eng.load(regs, base_row[0:1, bass.ds(first, GROUP)])
    return [eng.snap(r, min_val=0, max_val=N_NODES) for r in regs]


class Kept:

    def __init__(self, core, ctx):
        def sb(name, shape, dt=F32):
            return core.sb(ctx, name, shape, dt)

        self.ident = sb("ident", [P, P])
        self.iota = sb("iota", [P, P])
        self.iota_p = sb("iota_p", [P, 1])
        self.src = sb("src_index", [P, CHUNKS + RING * GROUP], I32)
        self.local = sb("local_dst", [P, CHUNKS + HALF])
        self.base_row = sb("base_row", [1, CHUNKS], I32)
        self.dinv = sb("dinv", [P, TILES])
        self.deg_inv = sb("deg_inv", [P, TILES])

        self.goes_on, self.stays, self.ends, self.reset = (
            sb(n, [ROWS, SUPERS, P], BF16) for n in ("goes_on", "stays", "ends", "reset"))
        self.row_goes_on, self.row_stays, self.row_reset = (
            sb(n, [HEADS, SUPERS, ROWS], BF16) for n in ("row_goes_on", "row_stays", "row_reset"))
        self.heads_on = sb("heads_on", [HEADS, D])

        def dram(name, width, rows=N_PAD, dt=F32):
            return core.nc.dram_tensor(name, (rows, width), dt).ap()

        self.table0 = dram("hop1_table", D)
        self.table0b = dram("hop2_table", D)
        self.table1 = dram("l1_table", D + HEADS)
        self.dst1 = dram("l1_dst_table", HEADS)
        self.local_rows = dram("local_rows", P, CHUNKS, BF16)
        self.x1 = dram("x_after_l0", D)
        self.table2 = dram("l2_table", D + 1)
        self.x2 = dram("x_after_l1", D)
        self.table3 = dram("l3_table", 2 * D)
        self.dst3 = dram("l3_dst_table", D)
        self.x_skip = dram("x_and_skip", 2 * D)


def scale_nodes(core, k, table):
    nc = core.nc
    scaled, stored = core.sem("scale_done"), core.sem("scale_stored")
    with nc.Block() as block:
        @block.vector
        def _(dve):
            nc.vector.tensor_tensor(k.scaled[:], k.x[:], wide(k.dinv[:], D), ALU.mult).then_inc(scaled, 1)

        @block.sync
        def _(sp):
            sp.wait_ge(scaled, 1)
            sp.dma_start(table.rearrange("(t p) f -> p t f", p=P), k.scaled[:]).then_inc(stored, 16)
            sp.wait_ge(stored, 16)


def set_up(core, k, x, src_cols, dst_cols, base_row):
    nc = core.nc
    with ExitStack() as ctx:
        def sb(name, shape, dt=F32):
            return core.sb(ctx, name, shape, dt)

        dst_int = sb("dst_int", [P, CHUNKS], I32)
        lo_int = sb("lo_int", [P, CHUNKS], I32)
        hi_int = sb("hi_int", [P, CHUNKS], I32)
        dst_f = sb("dst_f", [P, CHUNKS])
        lo = sb("lo", [P, CHUNKS])
        hi = sb("hi", [P, CHUNKS])
        base_f = sb("base_f", [1, CHUNKS])
        ones = sb("ones", [1, P])
        iota_int = sb("iota_int", [P, P], I32)
        iota_p_int = sb("iota_p_int", [P, 1], I32)
        zeros = sb("zeros", [P, P], BF16)
        lo_hot = sb("lo_hot", [P, 2, GROUP, P], BF16)
        hi_hot = sb("hi_hot", [P, 2, GROUP, TILES], BF16)
        counts = sb("counts", [TILES, P])
        root = sb("root", [P, 2, TILES])
        seen = sb("seen", [P, TILES])
        base_ps = core.ps(ctx, "base_ps", [P, 2, 512])
        hist_ps = core.ps(ctx, "hist_ps", [P, 512])
        deg_ps = core.ps(ctx, "deg_ps", [P, 512])

        loaded = core.sem("setup_loaded")
        x_loaded = core.sem("setup_x_loaded")
        x_zeroed = core.sem("setup_x_zeroed")
        made = core.sem("setup_constants")
        ident_zeroed = core.sem("setup_ident_zeroed")
        step = core.sem("setup_vector_step")
        split = core.sem("setup_hi_lo")
        base_ready = core.sem("setup_base_ready")
        base_spread = core.sem("setup_base_spread")
        lo_ready = core.sem("setup_lo_hot")
        hi_ready = core.sem("setup_hi_hot")
        counted = core.sem("setup_counted")
        counts_ready = core.sem("setup_counts")
        deg_ready = core.sem("setup_deg")
        root_in = core.sem("setup_root_in")
        rooted = core.sem("setup_rooted")
        half = CHUNKS // 2

        block = ctx.enter_context(nc.Block())

        @block.sync
        def _(sp):
            sp.dma_start(dst_int[:], dst_cols).then_inc(loaded, 16)
            sp.dma_start(k.base_row[:], base_row).then_inc(loaded, 16)
            sp.dma_start(k.src[:, 0:CHUNKS], src_cols).then_inc(loaded, 16)
            sp.wait_ge(x_zeroed, 1)
            sp.dma_start(k.x[:, 0:FULL_TILES, :],
                         x[0:FULL_TILES * P, :].rearrange("(t p) f -> p t f", p=P)).then_inc(x_loaded, 16)
            sp.dma_start(k.x[0:TAIL, FULL_TILES, :], x[FULL_TILES * P:N_NODES, :]).then_inc(x_loaded, 16)
            sp.wait_ge(x_loaded, 32)

        @block.gpsimd
        def _(pool):
            nc.gpsimd.iota(iota_int[:], pattern=[[1, P]], base=0, channel_multiplier=0).then_inc(made, 1)
            nc.gpsimd.iota(iota_p_int[:], pattern=[[0, 1]], base=0, channel_multiplier=1).then_inc(made, 1)
            nc.gpsimd.memset(k.ident[:], 0.0).then_inc(ident_zeroed, 1)
            nc.gpsimd.memset(k.src[:, CHUNKS:], 0)
            nc.gpsimd.memset(k.x[:, FULL_TILES:TILES, :], 0.0).then_inc(x_zeroed, 1)
            pool.wait_ge(ident_zeroed, 1)
            nc.gpsimd.affine_select(out=k.ident[:], in_=k.ident[:], compare_op=ALU.not_equal, fill=1.0,
                                    base=0, pattern=[[-1, P]], channel_multiplier=1).then_inc(made, 1)

        @block.vector
        def _(dve):
            dve.wait_ge(made, 3)
            nc.vector.tensor_copy(k.iota[:], iota_int[:]).then_inc(step, 1)
            nc.vector.tensor_copy(k.iota_p[:], iota_p_int[:]).then_inc(step, 1)
            nc.vector.memset(ones[:], 1.0).then_inc(step, 1)
            nc.vector.memset(zeros[:], 0.0).then_inc(step, 1)
            dve.wait_ge(loaded, 48)
            nc.vector.tensor_copy(base_f[:], k.base_row[0:1, :]).then_inc(base_ready, 1)
            nc.vector.tensor_scalar(hi_int[:], dst_int[:], 7, None, ALU.logical_shift_right).then_inc(step, 1)
            nc.vector.tensor_scalar(lo_int[:], dst_int[:], P - 1, None, ALU.bitwise_and).then_inc(step, 1)
            nc.vector.tensor_copy(dst_f[:], dst_int[:]).then_inc(step, 1)
            nc.vector.memset(k.local[:, CHUNKS:], 0.0).then_inc(step, 1)
            dve.wait_ge(step, 8)
            nc.vector.tensor_copy(hi[:], hi_int[:]).then_inc(split, 1)
            nc.vector.tensor_copy(lo[:], lo_int[:]).then_inc(split, 1)
            dve.wait_ge(base_spread, 1)
            nc.vector.tensor_tensor(k.local[:, 0:CHUNKS].rearrange("p (a b) -> p a b", a=2),
                                    dst_f[:].rearrange("p (a b) -> p a b", a=2),
                                    base_ps[:, :, 0:half], ALU.subtract).then_inc(split, 1)
            dve.wait_ge(split, 3)
            with dve.Fori(0, GROUPS // 2) as i:
                for s in range(2):
                    dve.wait_ge(counted, i * 2 + (s + 1))
                    nc.vector.tensor_tensor(lo_hot[:, s, :, :],
                                            wide(lo[:, bass.ds(i * 16 + 8 * s, GROUP)], P),
                                            along(k.iota[:], GROUP), ALU.is_equal).then_inc(lo_ready, 1)
                    nc.vector.tensor_tensor(hi_hot[:, s, :, :],
                                            wide(hi[:, bass.ds(i * 16 + 8 * s, GROUP)], TILES),
                                            along(k.iota[:, 0:TILES], GROUP), ALU.is_equal).then_inc(hi_ready, 1)
            dve.wait_ge(counted, GROUPS + 2)
            nc.vector.tensor_copy(counts[:], hist_ps[0:TILES, 0:P]).then_inc(counts_ready, 1)
            dve.wait_ge(deg_ready, 1)
            nc.vector.tensor_scalar(root[:, 0, :], deg_ps[:, 0:TILES], 1.0, None, ALU.add).then_inc(root_in, 1)
            nc.vector.tensor_scalar(root[:, 1, :], deg_ps[:, 0:TILES], 1.0, None, ALU.max).then_inc(root_in, 1)
            nc.vector.tensor_scalar(seen[:], deg_ps[:, 0:TILES], 0.0, None, ALU.is_gt).then_inc(root_in, 1)
            dve.wait_ge(rooted, 1)
            nc.vector.reciprocal(k.dinv[:], root[:, 0, :]).then_inc(root_in, 1)
            nc.vector.reciprocal(root[:, 1, :], root[:, 1, :]).then_inc(root_in, 1)
            dve.wait_ge(root_in, 5)
            nc.vector.tensor_tensor(k.deg_inv[:], root[:, 1, :], seen[:], ALU.mult).then_inc(root_in, 1)

        @block.tensor
        def _(pe):
            pe.wait_ge(base_ready, 1)
            pe.wait_ge(step, 4)
            for h in range(2):
                mm = nc.tensor.matmul(base_ps[:, h, 0:half], ones[:], base_f[:, h * half:(h + 1) * half],
                                      start=True, stop=True)
            mm.then_inc(base_spread, 1)
            nc.tensor.matmul(hist_ps[0:TILES, 0:P], zeros[:, 0:TILES], zeros[:], start=True, stop=False,
                             skip_group_check=True).then_inc(counted, 2)
            with pe.Fori(0, GROUPS // 2) as i:
                for s in range(2):
                    pe.wait_ge(lo_ready, i * 2 + (s + 1))
                    pe.wait_ge(hi_ready, i * 2 + (s + 1))
                    for c in range(GROUP):
                        mm = nc.tensor.matmul(hist_ps[0:TILES, 0:P], hi_hot[:, s, c, :], lo_hot[:, s, c, :],
                                              start=False, stop=False, skip_group_check=True)
                    mm.then_inc(counted, 1)
            pe.wait_ge(counts_ready, 1)
            pe.wait_ge(made, 3)
            nc.tensor.transpose(deg_ps[:, 0:TILES], counts[:], k.ident[0:TILES, 0:TILES]).then_inc(deg_ready, 1)

        @block.scalar
        def _(act):
            act.wait_ge(root_in, 3)
            nc.scalar.activation(root[:], root[:], ACT.Sqrt).then_inc(rooted, 1)


def sum_over_edges(core, k, name, table, width, acc, kinds):
    nc = core.nc
    with ExitStack() as ctx:
        rows = core.sb(ctx, f"{name}_rows", [P, RING, GROUP, width])
        index = core.sb(ctx, f"{name}_index", [P, RING, GROUP], I32)
        hot = core.sb(ctx, f"{name}_hot", [P, 2, HALF, P])
        sums = [core.ps(ctx, f"{name}_sums{h}", [P, kinds, HALF, P]) for h in range(2)]

        staged = core.sem(f"{name}_index_staged")
        taken = core.sem(f"{name}_index_taken")
        landing = [core.sem(f"{name}_landing{r}") for r in range(RING)]
        hot_ready = core.sem(f"{name}_hot_ready")
        summed = core.sem(f"{name}_summed")
        added = core.sem(f"{name}_added")
        FREE, EMPTY = 2 * RING, 2 * HALF

        block = ctx.enter_context(nc.Block())

        @block.scalar
        def _(act):
            with act.Fori(0, ROUNDS) as i:
                for r in range(RING):
                    act.wait_ge(summed, i * 2 * RING + (2 * r + 2))
                    nc.scalar.copy(index[:, r, :], k.src[:, bass.ds(i * RING * GROUP + r * GROUP, GROUP)]
                                   ).then_inc(staged, 1)

        @block.gpsimd
        def _(pool):
            with pool.Fori(0, ROUNDS) as i:
                for r in range(RING):
                    pool.wait_ge(staged, i * RING + (r + 1))
                    pool.sem_inc(taken, 1)
                    for c in range(GROUP):
                        nc.gpsimd.indirect_dma_start(
                            out=rows[:, r, c, :], out_offset=None, in_=table,
                            in_offset=bass.IndirectOffsetOnAxis(ap=index[:, r, c:c + 1], axis=0),
                        ).then_inc(landing[r], 16)

        @block.tensor
        def _(pe):
            pe.sem_inc(summed, FREE)
            with pe.Fori(0, ROUNDS) as i:
                for r in range(RING):
                    pe.wait_ge(landing[r], i * 16 * GROUP + 16 * GROUP)
                    for h in range(2):
                        pe.wait_ge(hot_ready, i * 2 * RING + (2 * r + h + 1))
                        pe.wait_ge(added, i * 2 * RING * HALF + ((2 * r + h) * HALF + HALF))
                        for c in range(HALF):
                            row = rows[:, r, HALF * h + c, :]
                            mm = nc.tensor.matmul(sums[h][:, 0, c, :], row[:, 0:D], hot[:, h, c, :],
                                                  start=True, stop=True)
                            if kinds == 2:
                                mm = nc.tensor.matmul(sums[h][:, 1, c, :],
                                                      row[:, D:D + 1].to_broadcast([P, P]),
                                                      hot[:, h, c, :], start=True, stop=True)
                        mm.then_inc(summed, 1)

        @block.vector
        def _(dve):
            base = [dve.alloc_register(f"{name}_base{c}") for c in range(GROUP)]

            def make_hot(first, h):
                nc.vector.tensor_tensor(hot[:, h, :, :], wide(k.local[:, bass.ds(first, HALF)], P),
                                        along(k.iota[:], HALF), ALU.is_equal).then_inc(hot_ready, 1)

            nc.vector.memset(acc, 0.0).then_inc(added, EMPTY)
            make_hot(0, 0)
            with dve.Fori(0, ROUNDS) as i:
                for r in range(RING):
                    first_node = load_bases(dve, base, k.base_row, i * RING * GROUP + r * GROUP)
                    for h in range(2):
                        n = 2 * r + h
                        dve.wait_ge(summed, i * 2 * RING + (FREE + n))
                        make_hot(i * RING * GROUP + (n + 1) * HALF, 1 - h)
                        dve.wait_ge(summed, i * 2 * RING + (FREE + n + 1))
                        for c in range(HALF):
                            dve.wait_ge(added, i * 2 * RING * HALF + (EMPTY + n * HALF + c))
                            at = first_node[HALF * h + c]
                            window = acc[:, :, bass.ds(at, P)]
                            nc.vector.tensor_tensor(window, window, sums[h][:, :, c, :], ALU.add
                                                    ).then_inc(added, 1)
            dve.wait_ge(added, EMPTY + CHUNKS)


class Steps:

    def __init__(self, core, name, steps):
        self.sem, self.steps = core.sem(name), steps

    def start(self, eng):
        eng.sem_inc(self.sem, self.steps)

    def wait(self, eng, i, step):
        eng.wait_ge(self.sem, i * self.steps + (self.steps + step))

    def wait_before(self, eng, i, step):
        eng.wait_ge(self.sem, i * self.steps + step)


def rows_of(dram, i):
    return dram[bass.ds(i * (QUAD * P), QUAD * P), :].rearrange("(t p) f -> p t f", p=P)


def propagate_nodes(core, k, acc, table):
    nc = core.nc
    with ExitStack() as ctx:
        features = core.sb(ctx, "hop_features", [P, QUAD * P])
        weighted = core.sb(ctx, "hop_weighted", [P, QUAD, D])
        c_acc = core.sb(ctx, "hop_c_acc", [P, TILES])
        c_self = core.sb(ctx, "hop_c_self", [P, TILES])
        nodes = core.ps(ctx, "hop_nodes", [P, QUAD, D])
        copied = Steps(core, "hop_copied", 1)
        turned = Steps(core, "hop_turned", 1)
        mixed = Steps(core, "hop_mixed", 3)
        stored = core.sem("hop_stored")
        coeff = core.sem("hop_coefficients")
        block = ctx.enter_context(nc.Block())

        @block.scalar
        def _(act):
            copied.start(act)
            with act.Fori(0, QUADS) as i:
                turned.wait_before(act, i, 1)
                nc.scalar.copy(features[:], acc[:, 0, bass.ds(i * (QUAD * P), QUAD * P)]).then_inc(copied.sem, 1)

        @block.tensor
        def _(pe):
            turned.start(pe)
            with pe.Fori(0, QUADS) as i:
                copied.wait(pe, i, 1)
                mixed.wait_before(pe, i, 1)
                for t in range(QUAD):
                    mm = nc.tensor.transpose(nodes[:, t, :], features[:, t * P:(t + 1) * P], k.ident[:])
                mm.then_inc(turned.sem, 1)

        @block.vector
        def _(dve):
            mixed.start(dve)
            nc.vector.scalar_tensor_tensor(out=c_acc[:], in0=k.dinv[:], scalar=0.5, in1=k.dinv[:],
                                           op0=ALU.mult, op1=ALU.mult).then_inc(coeff, 1)
            dve.wait_ge(coeff, 1)
            nc.vector.tensor_scalar(c_self[:], c_acc[:], 0.5, None, ALU.add).then_inc(coeff, 1)
            dve.wait_ge(coeff, 2)
            with dve.Fori(0, QUADS) as i:
                scaled = k.scaled[:, bass.ds(i * QUAD, QUAD), :]
                turned.wait(dve, i, 1)
                nc.vector.tensor_tensor(weighted[:], nodes[:], wide(c_acc[:, bass.ds(i * QUAD, QUAD)], D),
                                        ALU.mult).then_inc(mixed.sem, 1)
                nc.vector.tensor_tensor(scaled, scaled, wide(c_self[:, bass.ds(i * QUAD, QUAD)], D),
                                        ALU.mult).then_inc(mixed.sem, 1)
                mixed.wait(dve, i, 2)
                nc.vector.tensor_tensor(scaled, scaled, weighted[:], ALU.add).then_inc(mixed.sem, 1)
                mixed.wait(dve, i, 3)

        @block.sync
        def _(sp):
            with sp.Fori(0, QUADS) as i:
                mixed.wait(sp, i, 3)
                sp.dma_start(rows_of(table, i), k.scaled[:, bass.ds(i * QUAD, QUAD), :]).then_inc(stored, 16)
            sp.wait_ge(stored, 16 * QUADS)


class Norm:
    VECTOR_STEPS = 4 * QUAD // QUAD

    def __init__(self, core, ctx, name, z):
        self.nc, self.z = core.nc, z
        self.stats = core.sb(ctx, f"{name}_stats", [P, QUAD, 6])
        self.mean_var = core.sb(ctx, f"{name}_mean_var", [P, QUAD, 2])
        self.deviation = core.sb(ctx, f"{name}_deviation", [P, QUAD])
        self.held = core.sem(f"{name}_held")
        self.eps = core.sb(ctx, f"{name}_eps", [P, 1])

    def vector(self, dve, i, vector, v, scalar, s):
        nc = self.nc
        vector.wait(dve, i, v)
        for t in range(QUAD):
            last = nc.vector.bn_stats(self.stats[:, t, :], self.z[:, t, :])
        last.then_inc(vector.sem, 1)
        vector.wait(dve, i, v + 1)
        dve.sem_inc(self.held, 1)
        for t in range(QUAD):
            last = nc.vector.bn_aggr(self.mean_var[:, t, :], self.stats[:, t, :])
        last.then_inc(vector.sem, 1)
        scalar.wait(dve, i, s)
        nc.vector.reciprocal(self.deviation[:], self.deviation[:]).then_inc(vector.sem, 1)
        vector.wait(dve, i, v + 3)
        for t in range(QUAD):
            last = nc.vector.tensor_scalar(self.z[:, t, :], self.z[:, t, :], self.mean_var[:, t, 0:1],
                                           self.deviation[:, t:t + 1], ALU.subtract, ALU.mult)
        last.then_inc(vector.sem, 1)

    def scalar(self, act, i, vector, v, scalar):
        vector.wait(act, i, v + 2)
        self.nc.scalar.activation(self.deviation[:], self.mean_var[:, :, 1], ACT.Sqrt,
                                  bias=self.eps[:]).then_inc(scalar.sem, 1)


def leave_l0(core, k, ins, acc, x_out, table, dst_table):
    nc = core.nc
    WT = D + 2 * HEADS
    with ExitStack() as ctx:
        def sb(name, shape, dt=F32):
            return core.sb(ctx, f"l0_{name}", shape, dt)

        w1, w2t, w12 = sb("w1", [P, D]), sb("w2t", [P, D]), sb("w12", [P, D])
        b1, b2, b12 = sb("b1", [P, 1]), sb("b2", [1, D]), sb("b12", [1, D])
        ones = sb("ones", [1, P])
        w_heads = sb("w_heads", [P, WT])
        att = sb("att", [P, HEADS, 2, HC])
        product = sb("product", [P, HEADS, HC])
        half_dinv = sb("half_dinv", [P, TILES])
        features = sb("features", [P, QUAD * P])
        mix = sb("mix", [P, QUAD, D])
        relu_t = sb("relu_t", [P, QUAD * P])
        z = sb("z", [P, QUAD, D])
        z_t = sb("z_t", [P, QUAD * P])
        h = sb("h", [P, QUAD, WT])
        norm = Norm(core, ctx, "l0", z)
        w_ps = core.ps(ctx, "l0_w_ps", [P, 512])
        nodes = core.ps(ctx, "l0_nodes", [P, QUAD, D])
        turned_ps = core.ps(ctx, "l0_turned", [P, QUAD, D])
        out_ps = core.ps(ctx, "l0_out", [P, QUAD, D])
        h_ps = core.ps(ctx, "l0_heads_ps", [P, 2, 512])
        loaded = core.sem("l0_loaded")
        ready = core.sem("l0_weights_step")
        multiplied = core.sem("l0_weights_product")
        A = Steps(core, "l0_scalar", 5)
        T = Steps(core, "l0_tensor", 5)
        V = Steps(core, "l0_vector", 8)
        stored = Steps(core, "l0_stored", 48)
        READY = 10
        block = ctx.enter_context(nc.Block())

        @block.sync
        def _(sp):
            sp.dma_start(w1[:], ins["L0_gnn_w1"]).then_inc(loaded, 16)
            sp.dma_start(w2t[:], ins["w2_t"]).then_inc(loaded, 16)
            sp.dma_start(b1[:], ins["L0_gnn_b1"].rearrange("(p a) -> p a", a=1)).then_inc(loaded, 16)
            sp.dma_start(b2[:], ins["L0_gnn_b2"].rearrange("(a p) -> a p", a=1)).then_inc(loaded, 16)
            sp.dma_start(w_heads[:, 0:D], ins["L1_gnn_weight"]).then_inc(loaded, 16)
            sp.dma_start(att[:].rearrange("p h s c -> p (h s c)"),
                         ins["L1_gnn_att"].rearrange("a h c -> a (h c)").to_broadcast([P, 2 * D])).then_inc(loaded, 16)
            stored.start(sp)
            with sp.Fori(0, QUADS) as i:
                V.wait(sp, i, 8)
                sp.dma_start(rows_of(x_out, i), z[:]).then_inc(stored.sem, 16)
                A.wait(sp, i, 5)
                sp.dma_start(rows_of(table, i), h[:, :, 0:D + HEADS]).then_inc(stored.sem, 16)
                sp.dma_start(rows_of(dst_table, i), h[:, :, D + HEADS:WT]).then_inc(stored.sem, 16)
            stored.wait_before(sp, QUADS, 48)

        @block.vector
        def _(dve):
            V.start(dve)
            nc.vector.memset(ones[:], 1.0).then_inc(ready, 1)
            nc.vector.memset(norm.eps[:], EPS).then_inc(ready, 1)
            nc.vector.tensor_scalar(half_dinv[:], k.dinv[:], 0.5, None, ALU.mult).then_inc(ready, 1)
            dve.wait_ge(loaded, 96)
            heads = w_heads[:, 0:D].rearrange("p (h c) -> p h c", h=HEADS)
            for s in range(2):
                nc.vector.tensor_tensor(product[:], heads, att[:, :, s, :], ALU.mult).then_inc(ready, 1)
                dve.wait_ge(ready, 4 + 2 * s)
                nc.vector.tensor_reduce(w_heads[:, D + HEADS * s:D + HEADS * (s + 1)], product[:], AX_X,
                                        ALU.add).then_inc(ready, 1)
                dve.wait_ge(ready, 5 + 2 * s)
            dve.wait_ge(multiplied, 1)
            nc.vector.tensor_copy(w12[:], w_ps[:, 0:D]).then_inc(ready, 1)
            nc.vector.tensor_tensor(b12[:], w_ps[0:1, D:2 * D], b2[:], ALU.add).then_inc(ready, 1)
            dve.wait_ge(ready, READY - 1)
            nc.vector.memset(mix[:, 0, 0:1], 0.0).then_inc(ready, 1)
            dve.wait_ge(ready, READY)
            with dve.Fori(0, QUADS) as i:
                tiles = bass.ds(i * QUAD, QUAD)
                T.wait(dve, i, 1)
                nc.vector.tensor_tensor(mix[:], nodes[:], k.scaled[:, tiles, :], ALU.add).then_inc(V.sem, 1)
                V.wait(dve, i, 1)
                nc.vector.tensor_tensor(mix[:], mix[:], wide(half_dinv[:, tiles], D), ALU.mult).then_inc(V.sem, 1)
                V.wait(dve, i, 2)
                nc.vector.scalar_tensor_tensor(out=mix[:], in0=k.x[:, tiles, :], scalar=0.5, in1=mix[:],
                                               op0=ALU.mult, op1=ALU.add).then_inc(V.sem, 1)
                T.wait(dve, i, 3)
                stored.wait_before(dve, i, 48)
                nc.vector.tensor_tensor(z[:], out_ps[:], k.x[:, tiles, :], ALU.add).then_inc(V.sem, 1)
                norm.vector(dve, i, V, 4, A, 3)
                V.wait(dve, i, 8)

        @block.tensor
        def _(pe):
            T.start(pe)
            pe.wait_ge(loaded, 96)
            nc.tensor.matmul(w_ps[:, 0:D], w1[:], w2t[:], start=True, stop=True)
            nc.tensor.matmul(w_ps[0:1, D:2 * D], b1[:], w2t[:], start=True, stop=True).then_inc(multiplied, 1)
            pe.wait_ge(ready, READY)
            with pe.Fori(0, QUADS) as i:
                A.wait(pe, i, 1)
                for t in range(QUAD):
                    mm = nc.tensor.transpose(nodes[:, t, :], features[:, t * P:(t + 1) * P], k.ident[:])
                mm.then_inc(T.sem, 1)
                V.wait(pe, i, 3)
                for t in range(QUAD):
                    mm = nc.tensor.transpose(turned_ps[:, t, :], mix[:, t, :], k.ident[:])
                mm.then_inc(T.sem, 1)
                A.wait(pe, i, 2)
                for t in range(QUAD):
                    nc.tensor.matmul(out_ps[:, t, :], relu_t[:, t * P:(t + 1) * P], w12[:], start=True, stop=False)
                    mm = nc.tensor.matmul(out_ps[:, t, :], ones[:], b12[:], start=False, stop=True)
                mm.then_inc(T.sem, 1)
                V.wait(pe, i, 8)
                for t in range(QUAD):
                    mm = nc.tensor.transpose(turned_ps[:, t, :], z[:, t, :], k.ident[:])
                mm.then_inc(T.sem, 1)
                A.wait(pe, i, 4)
                for t in range(QUAD):
                    mm = nc.tensor.matmul(h_ps[:, t // 2, (t % 2) * WT:(t % 2 + 1) * WT],
                                          z_t[:, t * P:(t + 1) * P], w_heads[:], start=True, stop=True)
                mm.then_inc(T.sem, 1)

        @block.scalar
        def _(act):
            A.start(act)
            act.wait_ge(ready, READY)
            with act.Fori(0, QUADS) as i:
                T.wait_before(act, i, 1)
                nc.scalar.copy(features[:], acc[:, 0, bass.ds(i * (QUAD * P), QUAD * P)]).then_inc(A.sem, 1)
                T.wait(act, i, 2)
                nc.scalar.activation(relu_t[:].rearrange("p (t n) -> p t n", t=QUAD), turned_ps[:],
                                     ACT.Relu).then_inc(A.sem, 1)
                norm.scalar(act, i, V, 4, A)
                T.wait(act, i, 4)
                nc.scalar.copy(z_t[:].rearrange("p (t n) -> p t n", t=QUAD), turned_ps[:]).then_inc(A.sem, 1)
                T.wait(act, i, 5)
                stored.wait_before(act, i, 48)
                nc.scalar.copy(h[:].rearrange("p (a b) f -> p a (b f)", a=2), h_ps[:, :, 0:2 * WT]
                               ).then_inc(A.sem, 1)




def mark_segments(core, k, dst_line):
    nc = core.nc
    with ExitStack() as ctx:
        def sb(name, shape, dt=F32):
            return core.sb(ctx, f"mark_{name}", shape, dt)

        names = [sb(n, [ROWS, SUPERS, P], I32) for n in ("before", "here", "after")]
        values = [sb(n, [ROWS, SUPERS, P]) for n in ("before_f", "here_f", "after_f")]
        local = sb("local", [ROWS, SUPERS, P], BF16)
        row_keeps = sb("row_keeps", [ROWS, 2, SUPERS])
        level_ps = core.ps(ctx, "mark_level", [HEADS, 2, SUPERS, P])
        loaded, step, turned, stored = (core.sem(f"mark_{n}") for n in ("loaded", "step", "turned", "stored"))
        heads_cut = core.sem("mark_heads_cut")
        block = ctx.enter_context(nc.Block())

        @block.sync
        def _(sp):
            for n in range(3):
                sp.dma_start(names[n][:], dst_line[n:n + E_PAD].rearrange("(s p e) -> p s e", s=SUPERS, p=ROWS)
                             ).then_inc(loaded, 16)
            sp.wait_ge(step, 4)
            sp.dma_start(k.local_rows.rearrange("(s p) e -> p s e", p=ROWS), local[:]).then_inc(stored, 16)
            sp.wait_ge(stored, 16)

        @block.vector
        def _(dve):
            dve.wait_ge(loaded, 48)
            for n in range(3):
                nc.vector.tensor_copy(values[n][:], names[n][:]).then_inc(step, 1)
            dve.wait_ge(step, 3)
            before, here, after = (v[:] for v in values)
            first = values[1][:, :, 0:1].to_broadcast([ROWS, SUPERS, P])
            nc.vector.tensor_tensor(local[:], here, first, ALU.subtract).then_inc(step, 1)
            nc.vector.tensor_tensor(k.goes_on[:], here, before, ALU.is_equal).then_inc(step, 1)
            nc.vector.tensor_tensor(k.stays[:], here, after, ALU.is_equal).then_inc(step, 1)
            nc.vector.tensor_tensor(k.ends[:], here, after, ALU.not_equal).then_inc(step, 1)
            dve.wait_ge(step, 7)
            nc.vector.tensor_scalar(k.reset[:], k.goes_on[:], -1.0, BIG, ALU.add, ALU.mult).then_inc(step, 1)
            nc.vector.tensor_reduce(row_keeps[:, 0, :], k.goes_on[:], AX_X, ALU.min).then_inc(step, 1)
            nc.vector.tensor_reduce(row_keeps[:, 1, :], k.stays[:], AX_X, ALU.min).then_inc(step, 1)
            nc.vector.memset(k.heads_on[:], 1.0).then_inc(step, 1)
            dve.wait_ge(turned, 1)
            nc.vector.tensor_copy(k.row_goes_on[:], level_ps[:, 0, :, 0:ROWS]).then_inc(step, 1)
            nc.vector.tensor_copy(k.row_stays[:], level_ps[:, 1, :, 0:ROWS]).then_inc(step, 1)
            dve.wait_ge(step, 13)
            nc.vector.tensor_scalar(k.row_reset[:], k.row_goes_on[:], -1.0, BIG, ALU.add, ALU.mult
                                    ).then_inc(step, 1)

        @block.gpsimd
        def _(pool):
            pool.wait_ge(step, 11)
            nc.gpsimd.affine_select(out=k.heads_on[:], in_=k.heads_on[:], compare_op=ALU.is_ge, fill=0.0,
                                    base=0, pattern=[[1, D]], channel_multiplier=-HC).then_inc(heads_cut, 1)
            pool.wait_ge(heads_cut, 1)
            nc.gpsimd.affine_select(out=k.heads_on[:], in_=k.heads_on[:], compare_op=ALU.is_ge, fill=0.0,
                                    base=HC - 1, pattern=[[-1, D]], channel_multiplier=HC).then_inc(heads_cut, 1)

        @block.tensor
        def _(pe):
            pe.wait_ge(step, 10)
            for kind in range(2):
                for s in range(SUPERS):
                    keeps = row_keeps[:, kind, s:s + 1].to_broadcast([ROWS, HEADS])
                    mm = nc.tensor.transpose(level_ps[:, kind, s, 0:ROWS], keeps, k.ident[0:ROWS, 0:ROWS])
            mm.then_inc(turned, 1)


class SegmentSoftmax:

    VECTOR_STEPS = 33
    TENSOR_STEPS = 10
    SCALAR_STEPS = 3

    def __init__(self, core, k, ctx, name, scale):
        def sb(n, shape, dt=F32):
            return core.sb(ctx, f"{name}_{n}", shape, dt)

        self.nc, self.k, self.scale = core.nc, k, scale
        self.logits = sb("logits", [P, ROWS, HEADS])
        self.lg = sb("row_logits", [ROWS, HEADS, P])
        self.run = sb("running", [ROWS, HEADS, P])
        self.at_end = sb("at_end", [ROWS, HEADS, P])
        self.whole = sb("whole", [ROWS, HEADS, P])
        self.carried = sb("carried", [ROWS, HEADS])
        self.row_max = sb("row_max", [HEADS, ROWS + 1])
        self.row_sum = sb("row_sum", [HEADS, ROWS + 1])
        self.row_max_back = sb("row_max_back", [HEADS, ROWS + 1])
        self.row_sum_back = sb("row_sum_back", [HEADS, ROWS + 1])
        self.stays = sb("stays", [ROWS, P], BF16)
        self.row_stays = sb("row_stays", [HEADS, ROWS])
        self.held = core.sem(f"{name}_softmax_held")
        self.copied = core.sem(f"{name}_softmax_copied")
        self.shift = sb("shift", [HEADS, 1])
        self.factor = sb("factor", [HEADS, 1])
        self.weights = sb("weights", [P, HEADS, ROWS])
        self.rescale = sb("rescale", [P, 1])
        self.big_ps = core.ps(ctx, f"{name}_softmax_rows", [P, 512])
        self.small_ps = core.ps(ctx, f"{name}_softmax_level", [P, 512])
        self.V = Steps(core, f"{name}_softmax_vector", self.VECTOR_STEPS)
        self.T = Steps(core, f"{name}_softmax_tensor", self.TENSOR_STEPS)
        self.A = Steps(core, f"{name}_softmax_scalar", self.SCALAR_STEPS)
        self.emptied = core.sem(f"{name}_softmax_emptied")
        self.rows_ps = self.big_ps[0:ROWS, :].rearrange("p (h e) -> p h e", h=HEADS)
        self.level_ps = self.small_ps[0:HEADS, 0:ROWS]
        self.back_ps = self.small_ps[0:ROWS, P:P + HEADS]
        self.rescale_ps = self.small_ps[:, 2 * P:2 * P + 1]
        self.weights_ps = self.big_ps[:, 0:HEADS * ROWS].rearrange("p (h j) -> p h j", h=HEADS)

    def start_vector(self, dve):
        self.V.start(dve)
        self.nc.vector.memset(self.row_max[:, ROWS:], -BIG).then_inc(self.emptied, 1)
        self.nc.vector.memset(self.row_sum[:, ROWS:], 0.0).then_inc(self.emptied, 1)
        dve.wait_ge(self.emptied, 2)

    def vector(self, dve, s):
        nc, k, V, T, A = self.nc, self.k, self.V, self.T, self.A
        reset, goes_on, ends, row_reset, row_goes_on = (
            m[:, bass.ds(s, 1), :].rearrange("p a e -> p (a e)")
            for m in (k.reset, k.goes_on, k.ends, k.row_reset, k.row_goes_on))

        def scans(out, keep, x, initial, op0, op1, back=False):
            for h in range(HEADS):
                o, a, b = out[:, h, :], keep, x[:, h, :]
                if back:
                    o, a, b = o[:, ::-1], a[:, ::-1], b[:, ::-1]
                first = initial if isinstance(initial, float) else initial[:, h:h + 1]
                last = nc.vector.tensor_tensor_scan(out=o, data0=a, data1=b, initial=first, op0=op0, op1=op1)
            last.then_inc(V.sem, 1)

        def both_ways(x, level, level_back, keep, row_keep, empty, op0, op1, v, t):
            scans(self.run, keep, x, empty, op0, op1)
            T.wait(dve, s, t + 1)
            V.wait(dve, s, v)
            nc.vector.tensor_tensor_scan(out=level[:, 1:ROWS + 1], data0=row_keep, data1=self.level_ps,
                                         initial=level[:, 0:1], op0=op0, op1=op1).then_inc(V.sem, 1)
            T.wait(dve, s, t + 2)
            nc.vector.tensor_copy(self.carried[:], self.back_ps).then_inc(V.sem, 1)
            V.wait(dve, s, v + 3)
            scans(self.run, keep, x, self.carried, op0, op1)
            V.wait(dve, s, v + 4)
            nc.vector.tensor_tensor(self.at_end[:], self.run[:], along(ends, HEADS), ALU.mult).then_inc(V.sem, 1)
            V.wait(dve, s, v + 5)
            scans(self.whole, stays, self.at_end, 0.0, ALU.mult, ALU.add, back=True)
            T.wait(dve, s, t + 3)
            nc.vector.tensor_copy(level_back[:, ROWS:], level[:, ROWS:]).then_inc(V.sem, 1)
            V.wait(dve, s, v + 7)
            nc.vector.tensor_tensor_scan(out=level_back[:, 0:ROWS][:, ::-1], data0=row_stays[:, ::-1],
                                         data1=self.level_ps[:, ::-1], initial=level_back[:, ROWS:],
                                         op0=ALU.mult, op1=ALU.add).then_inc(V.sem, 1)
            T.wait(dve, s, t + 4)
            nc.vector.tensor_copy(self.carried[:], self.back_ps).then_inc(V.sem, 1)
            V.wait(dve, s, v + 9)
            scans(self.whole, stays, self.at_end, self.carried, ALU.mult, ALU.add, back=True)

        nc.vector.tensor_copy(self.stays[:], k.stays[:, bass.ds(s, 1), :].rearrange("p a e -> p (a e)")
                              ).then_inc(self.copied, 1)
        nc.vector.tensor_copy(self.row_stays[:], k.row_stays[:, bass.ds(s, 1), :].rearrange("p a e -> p (a e)")
                              ).then_inc(self.copied, 1)
        dve.wait_ge(self.copied, s * 2 + 2)
        stays, row_stays = self.stays[:], self.row_stays[:]
        nc.vector.tensor_copy(self.row_max[:, 0:1], self.row_max[:, ROWS:]).then_inc(V.sem, 1)
        A.wait(dve, s, 1)
        both_ways(self.lg, self.row_max, self.row_max_back, reset, row_reset, -BIG, ALU.add, ALU.max, 1, 1)
        nc.vector.tensor_tensor(self.shift[:], self.row_max[:, 0:1], self.row_max_back[:, 0:1],
                                ALU.subtract).then_inc(V.sem, 1)
        V.wait(dve, s, 12)
        nc.vector.tensor_scalar(self.shift[:], self.shift[:], 0.0, None, ALU.min).then_inc(V.sem, 1)
        nc.vector.tensor_tensor(self.lg[:], self.lg[:], self.whole[:], ALU.subtract).then_inc(V.sem, 1)
        A.wait(dve, s, 3)
        nc.vector.tensor_tensor(self.row_sum[:, 0:1], self.row_sum[:, ROWS:], self.factor[:],
                                ALU.mult).then_inc(V.sem, 1)
        both_ways(self.lg, self.row_sum, self.row_sum_back, goes_on, row_goes_on, 0.0, ALU.mult, ALU.add, 15, 5)
        V.wait(dve, s, 25)
        nc.vector.tensor_scalar(self.whole[:], self.whole[:], 1e-16, None, ALU.max).then_inc(V.sem, 1)
        nc.vector.tensor_scalar(self.factor[:], self.row_sum_back[:, 0:1], 1e-16, None, ALU.max
                                ).then_inc(V.sem, 1)
        V.wait(dve, s, 27)
        nc.vector.reciprocal(self.whole[:], self.whole[:]).then_inc(V.sem, 1)
        nc.vector.reciprocal(self.factor[:], self.factor[:]).then_inc(V.sem, 1)
        V.wait(dve, s, 29)
        nc.vector.tensor_tensor(self.lg[:], self.lg[:], self.whole[:], ALU.mult).then_inc(V.sem, 1)
        nc.vector.tensor_tensor(self.factor[:], self.factor[:], self.row_sum[:, 0:1], ALU.mult
                                ).then_inc(V.sem, 1)
        T.wait(dve, s, 10)
        nc.vector.tensor_copy(self.weights[:], self.weights_ps).then_inc(V.sem, 1)
        nc.vector.tensor_copy(self.rescale[:], self.rescale_ps).then_inc(V.sem, 1)
        V.wait(dve, s, 33)

    def tensor(self, pe, s):
        nc, k, V, T, A = self.nc, self.k, self.V, self.T, self.A
        V.wait_before(pe, s, self.VECTOR_STEPS)
        for h in range(HEADS):
            mm = nc.tensor.transpose(self.rows_ps[:, h, :], self.logits[:, :, h], k.ident[:])
        mm.then_inc(T.sem, 1)

        def both_ways(level, level_back, v):
            V.wait(pe, s, v + 1)
            nc.tensor.transpose(self.level_ps, self.run[:, :, P - 1], k.ident[0:ROWS, 0:ROWS]).then_inc(T.sem, 1)
            V.wait(pe, s, v + 2)
            pe.sem_inc(self.held, 1)
            nc.tensor.transpose(self.back_ps, level[:, 0:ROWS], k.ident[0:HEADS, 0:HEADS]).then_inc(T.sem, 1)
            V.wait(pe, s, v + 6)
            nc.tensor.transpose(self.level_ps, self.whole[:, :, 0], k.ident[0:ROWS, 0:ROWS]).then_inc(T.sem, 1)
            V.wait(pe, s, v + 8)
            pe.sem_inc(self.held, 1)
            nc.tensor.transpose(self.back_ps, level_back[:, 1:ROWS + 1], k.ident[0:HEADS, 0:HEADS]
                                ).then_inc(T.sem, 1)

        both_ways(self.row_max, self.row_max_back, 1)
        both_ways(self.row_sum, self.row_sum_back, 15)
        V.wait(pe, s, 31)
        nc.tensor.matmul(self.rescale_ps, k.heads_on[:], self.factor[:], start=True, stop=True)
        for h in range(HEADS):
            mm = nc.tensor.transpose(self.weights_ps[:, h, :], self.lg[:, h, :], k.ident[0:ROWS, 0:ROWS])
        mm.then_inc(T.sem, 1)

    def scalar(self, act, s):
        nc, V, T, A = self.nc, self.V, self.T, self.A
        T.wait(act, s, 1)
        nc.scalar.activation(self.lg[:], self.rows_ps, ACT.Copy, scale=self.scale).then_inc(A.sem, 1)
        V.wait(act, s, 13)
        nc.scalar.activation(self.factor[:], self.shift[:], ACT.Exp).then_inc(A.sem, 1)
        V.wait(act, s, 14)
        nc.scalar.activation(self.lg[:], self.lg[:], ACT.Exp).then_inc(A.sem, 1)


def attend(core, k, name, table, width, dst_table, dst_width, acc, scale, edge_attr_t=None, w_edge=None):
    nc = core.nc
    edges = edge_attr_t is not None
    LOOK = 4 if edges else 2
    with ExitStack() as ctx:
        def sb(n, shape, dt=F32):
            return core.sb(ctx, f"{name}_{n}", shape, dt)

        softmax = SegmentSoftmax(core, k, ctx, name, scale)
        rows = sb("rows", [P, RING, GROUP, width])
        kept = sb("kept", [P, ROWS, D])
        index = sb("index", [P, RING * GROUP], I32)
        target = sb("target", [P, 2 * HALF, dst_width])
        local_all = sb("local_all", [P, 2, HALF * P], BF16)
        distance = sb("distance", [P, 2, HALF * P])
        pick = sb("pick", [P, 2, HALF, P])
        hot = sb("hot", [P, 2, HALF, P])
        message = sb("message", [P, 2, HALF, D])
        minus_p = sb("minus_p", [P, 1])
        key = sb("key", [P, 2, HALF, D if edges else HEADS])
        attr = sb("attr", [EDGE_DIM, 2, HALF * P]) if edges else None
        we = sb("we", [EDGE_DIM, D]) if edges else None
        sums = [core.ps(ctx, f"{name}_sums{h}", [P, 1, HALF, P]) for h in range(2)]
        seen = [core.ps(ctx, f"{name}_seen{h}", [P, HALF, D]) for h in range(2)]
        edge_ps = [core.ps(ctx, f"{name}_edge{h}", [P, HALF, D]) for h in range(2)] if edges else None

        staged = core.sem(f"{name}_staged")
        taken = core.sem(f"{name}_taken")
        landing = [core.sem(f"{name}_landing{r}") for r in range(RING)]
        landed = core.sem(f"{name}_landed")
        windows = [core.sem(f"{name}_windows{h}") for h in range(2)]
        constant = core.sem(f"{name}_constant")
        we_loaded = core.sem(f"{name}_we_loaded")
        distance_ready = core.sem(f"{name}_distance")
        picked = core.sem(f"{name}_pick")
        values_kept = core.sem(f"{name}_values_kept")
        looked = core.sem(f"{name}_looked")
        logit = core.sem(f"{name}_logit_steps")
        prepared = core.sem(f"{name}_prepared")
        summed = core.sem(f"{name}_summed")
        added = core.sem(f"{name}_added")
        rescaled = core.sem(f"{name}_rescaled")
        EMPTY = 2 * HALF
        DMAS = HALF + (2 if edges else 1)

        block = ctx.enter_context(nc.Block())

        def over_supers(eng, superchunk):
            superchunk(0, True, False)
            with eng.Fori(1, SUPERS) as s:
                superchunk(s, True, True)
            superchunk(SUPERS, False, True)

        @block.gpsimd
        def _(pool):
            def gather(i):
                for r in range(RING):
                    pool.wait_ge(staged, i * RING + (r + 1))
                    pool.sem_inc(taken, 1)
                    for c in range(GROUP):
                        nc.gpsimd.indirect_dma_start(
                            out=rows[:, r, c, :], out_offset=None, in_=table,
                            in_offset=bass.IndirectOffsetOnAxis(ap=index[:, r * GROUP + c:r * GROUP + c + 1],
                                                                axis=0)).then_inc(landing[r], 16)
                    if r > 0:
                        pool.wait_ge(landing[r - 1], i * 16 * GROUP + 16 * GROUP)
                        pool.sem_inc(landed, 1)
                    elif not isinstance(i, int):
                        pool.wait_ge(landing[RING - 1], i * 16 * GROUP)
                        pool.sem_inc(landed, 1)

            gather(0)
            with pool.Fori(1, ROUNDS) as i:
                gather(i)
            pool.wait_ge(landing[RING - 1], ROUNDS * 16 * GROUP)
            pool.sem_inc(landed, 1)

        @block.sync
        def _(sp):
            base = [sp.alloc_register(f"{name}_sp_base{c}") for c in range(GROUP)]
            if edges:
                sp.dma_start(we[:], w_edge).then_inc(we_loaded, 16)
            with sp.Fori(0, GROUPS) as i:
                first_node = load_bases(sp, base, k.base_row, i * GROUP)
                for h in range(2):
                    sp.wait_ge(looked, i * 2 + (h + 1))
                    local = k.local_rows[bass.ds(i * GROUP + HALF * h, HALF), :]
                    sp.dma_start(local_all[:, h, :], local.rearrange("(a c) e -> a (c e)", a=1)
                                 .to_broadcast([P, HALF * P])).then_inc(windows[h], 16)
                    if edges:
                        sp.dma_start(attr[:, h, :], edge_attr_t[:, bass.ds(i * (GROUP * P) + HALF * h * P, HALF * P)]
                                     ).then_inc(windows[h], 16)
                    for c in range(HALF):
                        sp.dma_start(target[:, HALF * h + c, :],
                                     dst_table[bass.ds(first_node[HALF * h + c], P), :]).then_inc(windows[h], 16)

        @block.scalar
        def _(act):
            act.sem_inc(values_kept, 1)

            def stage(group, slot):
                nc.scalar.copy(index[:, bass.ds(slot * GROUP, GROUP)], k.src[:, bass.ds(group * GROUP, GROUP)]
                               ).then_inc(staged, 1)

            for g in range(RING - 1):
                stage(g, g)
            act.wait_ge(constant, 1)

            def superchunk(s, gathered, summing):
                if not gathered:
                    return
                with act.Fori(0, SUPER_GROUPS) as g:
                    G = act.snap(s * SUPER_GROUPS + g, min_val=0, max_val=GROUPS - 1)
                    act.wait_ge(logit, G * (2 * LOOK) + 2 * LOOK)
                    if not edges:
                        act.wait_ge(values_kept, G + 1)
                    stage(G + (RING - 1), act.snap((G + (RING - 1)) & (RING - 1), min_val=0, max_val=RING - 1))
                    for h in range(2):
                        act.wait_ge(windows[h], G * (16 * DMAS) + 16 * DMAS)
                        act.wait_ge(looked, G * 2 + (h + 1))
                        nc.scalar.activation(distance[:, h, :], local_all[:, h, :], ACT.Abs, bias=minus_p[:]
                                             ).then_inc(distance_ready, 1)
                        act.wait_ge(distance_ready, G * 2 + (h + 1))
                        nc.scalar.activation(pick[:, h, :, :].rearrange("p c e -> p (c e)"), distance[:, h, :],
                                             ACT.Relu, bias=1.0, scale=-1.0).then_inc(picked, 1)
                    if not edges:
                        act.wait_ge(landed, G + 1)
                        slot = act.snap(G & (RING - 1), min_val=0, max_val=RING - 1)
                        if summing:
                            act.wait_ge(prepared, (G - SUPER_GROUPS) * 4 + 4)
                        nc.scalar.copy(kept[:, bass.ds(g * GROUP, GROUP), :],
                                       rows[:, bass.ds(slot, 1), :, 0:D].rearrange("p a c f -> p (a c) f")
                                       ).then_inc(values_kept, 1)
                softmax.scalar(act, s)

            softmax.A.start(act)
            over_supers(act, superchunk)

        @block.tensor
        def _(pe):
            pe.sem_inc(looked, 2)
            pe.sem_inc(summed, 2)
            softmax.T.start(pe)
            if edges:
                pe.wait_ge(we_loaded, 16)

            def look(G, h):
                pe.wait_ge(windows[h], G * (16 * DMAS) + 16 * DMAS)
                pe.wait_ge(picked, G * 2 + (h + 1))
                pe.wait_ge(logit, G * (2 * LOOK) + (h + 1) * LOOK)
                for c in range(HALF):
                    mm = nc.tensor.matmul(seen[h][:, c, 0:dst_width], pick[:, h, c, :],
                                          target[:, HALF * h + c, :], start=True, stop=True)
                    if edges:
                        mm = nc.tensor.matmul(edge_ps[h][:, c, :], attr[:, h, c * P:(c + 1) * P], we[:],
                                              start=True, stop=True)
                mm.then_inc(looked, 1)

            def sum_up(G, h):
                pe.wait_ge(prepared, G * 4 + (2 * h + 2))
                pe.wait_ge(added, G * (2 * HALF) + (HALF * h + HALF))
                for c in range(HALF):
                    mm = nc.tensor.matmul(sums[h][:, 0, c, :], message[:, h, c, :], hot[:, h, c, :],
                                          start=True, stop=True)
                mm.then_inc(summed, 1)

            def superchunk(s, gathered, summing):
                with pe.Fori(0, SUPER_GROUPS) as g:
                    G = pe.snap(s * SUPER_GROUPS + g, min_val=0, max_val=GROUPS + SUPER_GROUPS - 1)
                    for h in range(2):
                        if gathered:
                            look(G, h)
                        if summing:
                            sum_up(G - SUPER_GROUPS, h)
                if gathered:
                    pe.wait_ge(logit, s * (SUPER_GROUPS * 2 * LOOK) + (SUPER_GROUPS * 2 + 2) * LOOK)
                    softmax.tensor(pe, s)

            over_supers(pe, superchunk)

        @block.vector
        def _(dve):
            base = [dve.alloc_register(f"{name}_base{c}") for c in range(GROUP)]
            nc.vector.tensor_scalar(minus_p[:], k.iota_p[:], -1.0, None, ALU.mult).then_inc(constant, 1)
            nc.vector.memset(acc, 0.0).then_inc(added, EMPTY)
            dve.sem_inc(logit, 2 * LOOK)
            softmax.start_vector(dve)

            def prepare(G, g, h):
                dve.wait_ge(summed, G * 2 + (h + 1))
                nc.vector.tensor_tensor(hot[:, h, :, :], wide(k.local[:, bass.ds(G * GROUP + HALF * h, HALF)], P),
                                        along(k.iota[:], HALF), ALU.is_equal).then_inc(prepared, 1)
                weight = softmax.weights[:, :, bass.ds(g * GROUP + HALF * h, HALF)].rearrange("p h j -> p j h")
                nc.vector.tensor_tensor(message[:, h, :, :].rearrange("p j (h c) -> p j h c", h=HEADS),
                                        kept[:, bass.ds(g * GROUP + HALF * h, HALF), :]
                                        .rearrange("p j (h c) -> p j h c", h=HEADS),
                                        weight.unsqueeze(3).to_broadcast([P, HALF, HEADS, HC]),
                                        ALU.mult).then_inc(prepared, 1)

            def look(G, g, h, slot, summing):
                dve.wait_ge(looked, G * 2 + (h + 3))
                row = rows[:, bass.ds(slot, 1), HALF * h:HALF * (h + 1), :].rearrange("p a c f -> p (a c) f")
                logits = softmax.logits[:, bass.ds(g * GROUP + HALF * h, HALF), :]
                done = G * (2 * LOOK) + (2 + h) * LOOK
                if not edges:
                    nc.vector.tensor_tensor(key[:, h, :, :], row[:, :, D:D + HEADS], seen[h][:, :, 0:HEADS],
                                            ALU.add).then_inc(logit, 1)
                    dve.wait_ge(logit, done + 1)
                    nc.vector.scalar_tensor_tensor(out=logits, in0=key[:, h, :, :], scalar=0.2,
                                                   in1=key[:, h, :, :], op0=ALU.mult, op1=ALU.max
                                                   ).then_inc(logit, 1)
                    return
                nc.vector.tensor_tensor(key[:, h, :, :], row[:, :, 0:D], edge_ps[h][:], ALU.add).then_inc(logit, 1)
                if summing:
                    dve.wait_ge(prepared, (G - SUPER_GROUPS) * 4 + (2 * h + 2))
                nc.vector.tensor_tensor(kept[:, bass.ds(g * GROUP + HALF * h, HALF), :], row[:, :, D:2 * D],
                                        edge_ps[h][:], ALU.add).then_inc(logit, 1)
                dve.wait_ge(logit, done + 1)
                nc.vector.tensor_tensor(key[:, h, :, :], key[:, h, :, :], seen[h][:], ALU.mult).then_inc(logit, 1)
                dve.wait_ge(logit, done + 3)
                nc.vector.tensor_reduce(logits, key[:, h, :, :].rearrange("p j (h c) -> p j h c", h=HEADS), AX_X,
                                        ALU.add).then_inc(logit, 1)

            def add(G, h, first_node):
                dve.wait_ge(summed, G * 2 + (h + 3))
                for c in range(HALF):
                    dve.wait_ge(added, G * (2 * HALF) + (EMPTY + HALF * h + c))
                    window = acc[:, :, bass.ds(first_node[HALF * h + c], P)]
                    nc.vector.tensor_tensor(window, window, sums[h][:, :, c, :], ALU.add).then_inc(added, 1)

            def superchunk(s, gathered, summing):
                with dve.Fori(0, SUPER_GROUPS) as g:
                    G = dve.snap(s * SUPER_GROUPS + g, min_val=0, max_val=GROUPS + SUPER_GROUPS - 1)
                    if gathered:
                        slot = dve.snap(G & (RING - 1), min_val=0, max_val=RING - 1)
                    if summing:
                        B = dve.snap(G - SUPER_GROUPS, min_val=0, max_val=GROUPS - 1)
                        first_node = load_bases(dve, base, k.base_row, B * GROUP)
                    for h in range(2):
                        if summing:
                            prepare(B, g, h)
                        if gathered:
                            if h == 0:
                                dve.wait_ge(landed, G + 1)
                            look(G, g, h, slot, summing)
                        if summing:
                            add(B, h, first_node)
                if gathered:
                    softmax.vector(dve, s)
                    dve.load([base[0]], k.base_row[0:1, bass.ds(s * ROWS, 1)])
                    node = dve.snap(base[0], min_val=0, max_val=N_NODES)
                    if summing:
                        dve.wait_ge(added, s * ROWS + EMPTY)
                    else:
                        dve.wait_ge(added, EMPTY)
                    column = acc[:, 0, bass.ds(node, 1)]
                    nc.vector.tensor_scalar(column, column, softmax.rescale[:], None, ALU.mult
                                            ).then_inc(rescaled, 1)
                    dve.wait_ge(rescaled, s + 1)

            over_supers(dve, superchunk)
            dve.wait_ge(added, EMPTY + CHUNKS)


def leave_l1(core, k, ins, acc, x_in, x_out, table):
    nc = core.nc
    with ExitStack() as ctx:
        def sb(name, shape, dt=F32):
            return core.sb(ctx, f"l1n_{name}", shape, dt)

        bias = sb("bias", [P, D])
        features = sb("features", [P, QUAD * P])
        x = sb("x", [P, QUAD, D])
        z = sb("z", [P, QUAD, D])
        weighted = sb("weighted", [P, QUAD, D + 1])
        norm = Norm(core, ctx, "l1n", z)
        nodes = core.ps(ctx, "l1n_nodes", [P, QUAD, D])
        loaded = core.sem("l1n_loaded")
        x_loaded = core.sem("l1n_x_loaded")
        ready = core.sem("l1n_eps")
        A = Steps(core, "l1n_scalar", 2)
        T = Steps(core, "l1n_tensor", 1)
        V = Steps(core, "l1n_vector", 8)
        stored = Steps(core, "l1n_stored", 32)
        block = ctx.enter_context(nc.Block())

        @block.sync
        def _(sp):
            sp.dma_start(bias[:], ins["L1_gnn_bias"].rearrange("(a f) -> a f", a=1).to_broadcast([P, D])
                         ).then_inc(loaded, 16)
            stored.start(sp)
            sp.dma_start(x[:], rows_of(x_in, 0)).then_inc(x_loaded, 16)

            def store(i):
                V.wait(sp, i, 8)
                sp.dma_start(rows_of(x_out, i), z[:]).then_inc(stored.sem, 16)
                sp.dma_start(rows_of(table, i), weighted[:]).then_inc(stored.sem, 16)

            with sp.Fori(1, QUADS) as i:
                V.wait_before(sp, i, 1)
                sp.dma_start(x[:], rows_of(x_in, i)).then_inc(x_loaded, 16)
                store(i - 1)
            store(QUADS - 1)
            stored.wait_before(sp, QUADS, 32)

        @block.vector
        def _(dve):
            V.start(dve)
            nc.vector.memset(norm.eps[:], EPS).then_inc(ready, 1)
            dve.wait_ge(loaded, 16)
            with dve.Fori(0, QUADS) as i:
                inverse = wide(k.deg_inv[:, bass.ds(i * QUAD, QUAD)], D)
                T.wait(dve, i, 1)
                dve.wait_ge(x_loaded, i * 16 + 16)
                stored.wait_before(dve, i, 32)
                nc.vector.tensor_tensor(z[:], nodes[:], x[:], ALU.add).then_inc(V.sem, 1)
                V.wait(dve, i, 1)
                nc.vector.tensor_tensor(z[:], z[:], along(bias[:], QUAD), ALU.add).then_inc(V.sem, 1)
                norm.vector(dve, i, V, 2, A, 2)
                V.wait(dve, i, 6)
                nc.vector.tensor_tensor(weighted[:, :, 0:D], z[:], inverse, ALU.mult).then_inc(V.sem, 1)
                nc.vector.tensor_copy(weighted[:, :, D:D + 1], wide(k.deg_inv[:, bass.ds(i * QUAD, QUAD)], 1)
                                      ).then_inc(V.sem, 1)

        @block.tensor
        def _(pe):
            T.start(pe)
            with pe.Fori(0, QUADS) as i:
                A.wait(pe, i, 1)
                V.wait_before(pe, i, 1)
                for t in range(QUAD):
                    mm = nc.tensor.transpose(nodes[:, t, :], features[:, t * P:(t + 1) * P], k.ident[:])
                mm.then_inc(T.sem, 1)

        @block.scalar
        def _(act):
            A.start(act)
            act.wait_ge(ready, 1)
            with act.Fori(0, QUADS) as i:
                T.wait_before(act, i, 1)
                nc.scalar.copy(features[:], acc[:, 0, bass.ds(i * (QUAD * P), QUAD * P)]).then_inc(A.sem, 1)
                norm.scalar(act, i, V, 2, A)


def leave_l2(core, k, ins, acc, x_in, table, dst_table, x_skip):
    nc = core.nc
    with ExitStack() as ctx:
        def sb(name, shape, dt=F32):
            return core.sb(ctx, f"l2_{name}", shape, dt)

        w3t = sb("w3t", [P, D])
        bias = sb("bias", [P, D])
        w_all = sb("w_all", [P, 4 * D])
        b_all = sb("b_all", [1, 4 * D])
        ones = sb("ones", [1, P])
        features = sb("features", [P, QUAD * P])
        counts = sb("counts", [1, QUAD * P])
        x = sb("x", [P, QUAD, D])
        cross = sb("cross", [P, QUAD, D])
        cross_t = sb("cross_t", [P, QUAD * P])
        z = sb("z", [P, QUAD, D])
        z_t = sb("z_t", [P, QUAD * P])
        n_sum = sb("n_sum", [P, QUAD])
        heads = sb("heads", [P, QUAD, 4 * D])
        norm = Norm(core, ctx, "l2", z)
        nodes = core.ps(ctx, "l2_nodes", [P, QUAD, D])
        turned_ps = core.ps(ctx, "l2_turned", [P, QUAD, D])
        out_ps = core.ps(ctx, "l2_out", [P, QUAD, D])
        n_ps = core.ps(ctx, "l2_n_ps", [P, 512])
        heads_ps = core.ps(ctx, "l2_heads_ps", [P, QUAD, 4 * D])
        loaded = core.sem("l2_loaded")
        x_loaded = core.sem("l2_x_loaded")
        ready = core.sem("l2_ready")
        A = Steps(core, "l2_scalar", 6)
        T = Steps(core, "l2_tensor", 5)
        V = Steps(core, "l2_vector", 12)
        stored = Steps(core, "l2_stored", 64)
        block = ctx.enter_context(nc.Block())

        @block.sync
        def _(sp):
            sp.dma_start(w3t[:], ins["w3_t"]).then_inc(loaded, 16)
            sp.dma_start(bias[:], ins["L2_gnn_W1_b"].rearrange("(a f) -> a f", a=1).to_broadcast([P, D])
                         ).then_inc(loaded, 16)
            for n, part in enumerate(("k", "v", "q", "skip")):
                sp.dma_start(w_all[:, n * D:(n + 1) * D], ins[f"L3_gnn_W{part}"]).then_inc(loaded, 16)
                sp.dma_start(b_all[:, n * D:(n + 1) * D], ins[f"L3_gnn_b{part}"].rearrange("(a f) -> a f", a=1)
                             ).then_inc(loaded, 16)
            stored.start(sp)
            sp.dma_start(x[:], rows_of(x_in, 0)).then_inc(x_loaded, 16)

            def store(i):
                V.wait(sp, i, 12)
                sp.dma_start(rows_of(x_skip[:, 0:D], i), z[:]).then_inc(stored.sem, 16)
                A.wait(sp, i, 6)
                sp.dma_start(rows_of(table, i), heads[:, :, 0:2 * D]).then_inc(stored.sem, 16)
                sp.dma_start(rows_of(dst_table, i), heads[:, :, 2 * D:3 * D]).then_inc(stored.sem, 16)
                sp.dma_start(rows_of(x_skip[:, D:2 * D], i), heads[:, :, 3 * D:]).then_inc(stored.sem, 16)

            with sp.Fori(1, QUADS) as i:
                V.wait_before(sp, i, 8)
                sp.dma_start(x[:], rows_of(x_in, i)).then_inc(x_loaded, 16)
                store(i - 1)
            store(QUADS - 1)
            stored.wait_before(sp, QUADS, 64)

        @block.vector
        def _(dve):
            V.start(dve)
            nc.vector.memset(norm.eps[:], EPS).then_inc(ready, 1)
            nc.vector.memset(ones[:], 1.0).then_inc(ready, 1)
            dve.wait_ge(loaded, 160)
            with dve.Fori(0, QUADS) as i:
                T.wait(dve, i, 1)
                dve.wait_ge(x_loaded, i * 16 + 16)
                nc.vector.tensor_tensor(cross[:], nodes[:], x[:], ALU.mult).then_inc(V.sem, 1)
                nc.vector.tensor_copy(n_sum[:], n_ps[:, 0:QUAD]).then_inc(V.sem, 1)
                stored.wait_before(dve, i, 64)
                nc.vector.tensor_tensor(z[:], x[:], along(bias[:], QUAD), ALU.add).then_inc(V.sem, 1)
                V.wait(dve, i, 3)
                nc.vector.tensor_tensor(z[:], z[:], wide(n_sum[:], D), ALU.mult).then_inc(V.sem, 1)
                V.wait(dve, i, 4)
                T.wait(dve, i, 3)
                nc.vector.tensor_tensor(z[:], z[:], out_ps[:], ALU.add).then_inc(V.sem, 1)
                V.wait(dve, i, 5)
                nc.vector.tensor_tensor(z[:], z[:], wide(k.deg_inv[:, bass.ds(i * QUAD, QUAD)], D), ALU.mult
                                        ).then_inc(V.sem, 1)
                V.wait(dve, i, 6)
                nc.vector.scalar_tensor_tensor(out=z[:], in0=z[:], scalar=0.01, in1=z[:], op0=ALU.mult,
                                               op1=ALU.max).then_inc(V.sem, 1)
                V.wait(dve, i, 7)
                nc.vector.tensor_tensor(z[:], z[:], x[:], ALU.add).then_inc(V.sem, 1)
                norm.vector(dve, i, V, 8, A, 4)

        @block.tensor
        def _(pe):
            T.start(pe)
            pe.wait_ge(loaded, 160)
            pe.wait_ge(ready, 2)
            with pe.Fori(0, QUADS) as i:
                A.wait(pe, i, 2)
                V.wait_before(pe, i, 2)
                for t in range(QUAD):
                    nc.tensor.transpose(nodes[:, t, :], features[:, t * P:(t + 1) * P], k.ident[:])
                for t in range(QUAD):
                    mm = nc.tensor.transpose(n_ps[:, t:t + 1], counts[:, t * P:(t + 1) * P], k.ident[0:1, 0:1])
                mm.then_inc(T.sem, 1)
                V.wait(pe, i, 1)
                for t in range(QUAD):
                    mm = nc.tensor.transpose(turned_ps[:, t, :], cross[:, t, :], k.ident[:])
                mm.then_inc(T.sem, 1)
                A.wait(pe, i, 3)
                for t in range(QUAD):
                    mm = nc.tensor.matmul(out_ps[:, t, :], cross_t[:, t * P:(t + 1) * P], w3t[:],
                                          start=True, stop=True)
                mm.then_inc(T.sem, 1)
                V.wait(pe, i, 12)
                for t in range(QUAD):
                    mm = nc.tensor.transpose(turned_ps[:, t, :], z[:, t, :], k.ident[:])
                mm.then_inc(T.sem, 1)
                A.wait(pe, i, 5)
                for t in range(QUAD):
                    nc.tensor.matmul(heads_ps[:, t, :], z_t[:, t * P:(t + 1) * P], w_all[:], start=True, stop=False)
                    mm = nc.tensor.matmul(heads_ps[:, t, :], ones[:], b_all[:], start=False, stop=True)
                mm.then_inc(T.sem, 1)

        @block.scalar
        def _(act):
            A.start(act)
            act.wait_ge(ready, 1)
            with act.Fori(0, QUADS) as i:
                T.wait_before(act, i, 1)
                nc.scalar.copy(features[:], acc[:, 0, bass.ds(i * (QUAD * P), QUAD * P)]).then_inc(A.sem, 1)
                nc.scalar.copy(counts[:], acc[0:1, 1, bass.ds(i * (QUAD * P), QUAD * P)]).then_inc(A.sem, 1)
                T.wait(act, i, 2)
                nc.scalar.copy(cross_t[:].rearrange("p (t n) -> p t n", t=QUAD), turned_ps[:]).then_inc(A.sem, 1)
                norm.scalar(act, i, V, 8, A)
                T.wait(act, i, 4)
                nc.scalar.copy(z_t[:].rearrange("p (t n) -> p t n", t=QUAD), turned_ps[:]).then_inc(A.sem, 1)
                T.wait(act, i, 5)
                stored.wait_before(act, i, 64)
                nc.scalar.copy(heads[:], heads_ps[:]).then_inc(A.sem, 1)


def leave_l3(core, k, acc, x_skip, out):
    nc = core.nc
    with ExitStack() as ctx:
        def sb(name, shape, dt=F32):
            return core.sb(ctx, f"l3n_{name}", shape, dt)

        features = sb("features", [P, QUAD * P])
        x = sb("x", [P, QUAD, 2 * D])
        z = sb("z", [P, QUAD, D])
        norm = Norm(core, ctx, "l3n", z)
        nodes = core.ps(ctx, "l3n_nodes", [P, QUAD, D])
        x_loaded = core.sem("l3n_x_loaded")
        ready = core.sem("l3n_eps")
        A = Steps(core, "l3n_scalar", 2)
        T = Steps(core, "l3n_tensor", 1)
        V = Steps(core, "l3n_vector", 6)
        stored = Steps(core, "l3n_stored", 16)
        block = ctx.enter_context(nc.Block())

        @block.sync
        def _(sp):
            stored.start(sp)
            sp.dma_start(x[:], rows_of(x_skip, 0)).then_inc(x_loaded, 16)
            with sp.Fori(1, QUADS) as i:
                V.wait_before(sp, i, 2)
                sp.dma_start(x[:], rows_of(x_skip, i)).then_inc(x_loaded, 16)
                V.wait_before(sp, i, 6)
                sp.dma_start(rows_of(out, i - 1), z[:]).then_inc(stored.sem, 16)
            V.wait(sp, QUADS - 1, 6)
            sp.dma_start(out[FULL_TILES * P:N_NODES, :], z[0:TAIL, 0, :]).then_inc(stored.sem, 16)
            stored.wait_before(sp, QUADS, 16)

        @block.vector
        def _(dve):
            V.start(dve)
            nc.vector.memset(norm.eps[:], EPS).then_inc(ready, 1)
            with dve.Fori(0, QUADS) as i:
                T.wait(dve, i, 1)
                dve.wait_ge(x_loaded, i * 16 + 16)
                stored.wait_before(dve, i, 16)
                nc.vector.tensor_tensor(z[:], nodes[:], x[:, :, D:2 * D], ALU.add).then_inc(V.sem, 1)
                V.wait(dve, i, 1)
                nc.vector.scalar_tensor_tensor(out=z[:], in0=z[:], scalar=0.0, in1=x[:, :, 0:D], op0=ALU.max,
                                               op1=ALU.add).then_inc(V.sem, 1)
                norm.vector(dve, i, V, 2, A, 2)

        @block.tensor
        def _(pe):
            T.start(pe)
            with pe.Fori(0, QUADS) as i:
                A.wait(pe, i, 1)
                V.wait_before(pe, i, 1)
                for t in range(QUAD):
                    mm = nc.tensor.transpose(nodes[:, t, :], features[:, t * P:(t + 1) * P], k.ident[:])
                mm.then_inc(T.sem, 1)

        @block.scalar
        def _(act):
            A.start(act)
            act.wait_ge(ready, 1)
            with act.Fori(0, QUADS) as i:
                T.wait_before(act, i, 1)
                nc.scalar.copy(features[:], acc[:, 0, bass.ds(i * (QUAD * P), QUAD * P)]).then_inc(A.sem, 1)
                norm.scalar(act, i, V, 2, A)


def build(nc, ins, out):
    core = Core(nc)
    with ExitStack() as ctx:
        k = Kept(core, ctx)
        with ExitStack() as l0:
            k.x = core.sb(l0, "x_nodes", [P, TILES, D])
            k.scaled = core.sb(l0, "x_scaled", [P, TILES, D])
            acc = core.sb(l0, "l0_acc", [P, 1, N_PAD])
            set_up(core, k, ins["x"], ins["src_cols"], ins["dst_cols"], ins["base_row"])
            scale_nodes(core, k, k.table0)
            sum_over_edges(core, k, "hop1", k.table0, D, acc[:], 1)
            propagate_nodes(core, k, acc, k.table0b)
            sum_over_edges(core, k, "hop2", k.table0b, D, acc[:], 1)
            leave_l0(core, k, ins, acc, k.x1, k.table1, k.dst1)
        mark_segments(core, k, ins["dst_line"])
        with ExitStack() as l1:
            acc = core.sb(l1, "l1_acc", [P, 1, N_PAD])
            attend(core, k, "l1", k.table1, D + HEADS, k.dst1, HEADS, acc[:], 1.0)
            leave_l1(core, k, ins, acc, k.x1, k.x2, k.table2)
        with ExitStack() as l2:
            acc = core.sb(l2, "l2_acc", [P, 2, N_PAD])
            sum_over_edges(core, k, "l2", k.table2, D + 1, acc[:], 2)
            leave_l2(core, k, ins, acc, k.x2, k.table3, k.dst3, k.x_skip)
        with ExitStack() as l3:
            acc = core.sb(l3, "l3_acc", [P, 1, N_PAD])
            attend(core, k, "l3", k.table3, 2 * D, k.dst3, D, acc[:], float(HC) ** -0.5,
                   ins["edge_attr_t"], ins["L3_gnn_We"])
            leave_l3(core, k, acc, k.x_skip, out)


def kernel(**inputs):
    import concourse.bacc as bacc
    from concourse.bass_utils import run_bass_kernel_spmd

    nc = bacc.Bacc("TRN2", target_bir_lowering=False, num_devices=1)
    src = np.asarray(inputs["src"])
    dst = np.asarray(inputs["dst"])
    pad = E_PAD - N_EDGES
    src = np.concatenate([src, np.zeros(pad, src.dtype)])
    dst = np.concatenate([np.full(1, -1, dst.dtype), dst, np.full(pad + 1, N_NODES, dst.dtype)])
    arrays = {name: np.ascontiguousarray(a) for name, a in inputs.items()
              if name not in ("src", "dst", "edge_attr_32", "edge_weight")}
    arrays["src_cols"] = np.ascontiguousarray(src.reshape(CHUNKS, CHUNK).T)
    arrays["dst_cols"] = np.ascontiguousarray(dst[1:-1].reshape(CHUNKS, CHUNK).T)
    arrays["base_row"] = np.ascontiguousarray(dst[1:-1:CHUNK].reshape(1, CHUNKS))
    arrays["dst_line"] = dst
    arrays["w2_t"] = np.ascontiguousarray(arrays.pop("L0_gnn_w2").T)
    arrays["w3_t"] = np.ascontiguousarray(arrays.pop("L2_gnn_W1_w").T)
    edge_attr = np.asarray(inputs["edge_attr_32"])
    arrays["edge_attr_t"] = np.ascontiguousarray(
        np.concatenate([edge_attr, np.zeros((pad, EDGE_DIM), edge_attr.dtype)]).T)
    ins = {name: nc.dram_tensor(f"in_{name}", a.shape, mybir.dt.from_np(a.dtype), kind="ExternalInput").ap()
           for name, a in arrays.items()}
    out = nc.dram_tensor("out", (N_NODES, D), F32, kind="ExternalOutput").ap()
    build(nc, ins, out)
    r = run_bass_kernel_spmd(nc, [{f"in_{name}": a for name, a in arrays.items()}], core_ids=[0])
    return r.results[0]["out"]
```

```python
from contextlib import ExitStack

import numpy as np
import concourse.bass as bass
import concourse.mybir as mybir

F32 = mybir.dt.float32
BF16 = mybir.dt.bfloat16
I32 = mybir.dt.int32
ALU = mybir.AluOpType
ACT = mybir.ActivationFunctionType
AX_X = mybir.AxisListType.X

P = 128
N_NODES = 6250
N_EDGES = 106250
D = 128
HEADS = 4
HC = D // HEADS
EDGE_DIM = 32

CHUNK = P
GROUP = 8
CHUNKS = -(-N_EDGES // (CHUNK * GROUP)) * GROUP
GROUPS = CHUNKS // GROUP
E_PAD = CHUNKS * CHUNK
RING = 4
ROUNDS = GROUPS // RING
LONG_RING = 8
HALF = GROUP // 2
TILES = 52
N_PAD = TILES * P
QUAD = 4
QUADS = TILES // QUAD
FULL_TILES, TAIL = divmod(N_NODES, P)
EPS = 1e-5
SUPERS = 8
ROWS = CHUNKS // SUPERS
SUPER_GROUPS = ROWS // GROUP
BIG = 1e30
assert ROWS * SUPERS == CHUNKS and SUPER_GROUPS * GROUP == ROWS
assert CHUNKS == ROUNDS * RING * GROUP and TILES == QUADS * QUAD


class Core:

    def __init__(self, nc):
        self.nc = nc
        self.held = nc.alloc_semaphore("held")

    def sb(self, ctx, name, shape, dt=F32):
        return ctx.enter_context(self.nc.sbuf_tensor(name, shape, dt))

    def ps(self, ctx, name, shape):
        return ctx.enter_context(self.nc.psum_tensor(name, shape, F32))

    def sem(self, name):
        return self.nc.alloc_semaphore(name)

    def hold(self, eng):
        eng.sem_inc(self.held, 1)


def wide(ap, n):
    return ap.unsqueeze(2).to_broadcast([ap.shape[0], ap.shape[1], n])


def along(ap, k):
    return ap.unsqueeze(1).to_broadcast([ap.shape[0], k, ap.shape[1]])


def load_bases(eng, regs, base_row, first):
    eng.load(regs, base_row[0:1, bass.ds(first, len(regs))])
    return [eng.snap(r, min_val=0, max_val=N_NODES) for r in regs]


class Kept:

    def __init__(self, core, ctx):
        def sb(name, shape, dt=F32):
            return core.sb(ctx, name, shape, dt)

        self.ident = sb("ident", [P, P])
        self.iota = sb("iota", [P, P])
        self.iota_p = sb("iota_p", [P, 1])
        self.src = sb("src_index", [P, CHUNKS + LONG_RING * GROUP], I32)
        self.local = sb("local_dst", [P, CHUNKS + GROUP])
        self.base_row = sb("base_row", [1, CHUNKS], I32)
        self.dinv = sb("dinv", [P, TILES])
        self.deg_inv = sb("deg_inv", [P, TILES])

        self.goes_on, self.stays, self.ends, self.reset = (
            sb(n, [ROWS, SUPERS, P], BF16) for n in ("goes_on", "stays", "ends", "reset"))
        self.row_goes_on, self.row_stays, self.row_reset = (
            sb(n, [HEADS, SUPERS, ROWS], BF16) for n in ("row_goes_on", "row_stays", "row_reset"))
        self.heads_on = sb("heads_on", [HEADS, D])

        self.landing = [core.sem(f"landing{r}") for r in range(RING)]
        self.landed = 0

        def dram(name, width, rows=N_PAD, dt=F32):
            return core.nc.dram_tensor(name, (rows, width), dt).ap()

        self.table0 = dram("hop1_table", D)
        self.table0b = dram("hop2_table", D)
        self.table1 = dram("l1_table", D + HEADS)
        self.dst1 = dram("l1_dst_table", HEADS)
        self.local_rows = dram("local_rows", P, CHUNKS, BF16)
        self.x1 = dram("x_after_l0", D)
        self.table2 = dram("l2_table", D + 1)
        self.x2 = dram("x_after_l1", D)
        self.table3 = dram("l3_table", 2 * D)
        self.dst3 = dram("l3_dst_table", D)
        self.x_skip = dram("x_and_skip", 2 * D)


def scale_nodes(core, k, table):
    nc = core.nc
    scaled, stored = core.sem("scale_done"), core.sem("scale_stored")
    with nc.Block() as block:
        @block.vector
        def _(dve):
            nc.vector.tensor_tensor(k.scaled[:], k.x[:], wide(k.dinv[:], D), ALU.mult).then_inc(scaled, 1)

        @block.sync
        def _(sp):
            sp.wait_ge(scaled, 1)
            sp.dma_start(table.rearrange("(t p) f -> p t f", p=P), k.scaled[:]).then_inc(stored, 16)
            sp.wait_ge(stored, 16)


def set_up(core, k, x, src_cols, dst_cols, base_row):
    nc = core.nc
    with ExitStack() as ctx:
        def sb(name, shape, dt=F32):
            return core.sb(ctx, name, shape, dt)

        dst_int = sb("dst_int", [P, CHUNKS], I32)
        lo_int = sb("lo_int", [P, CHUNKS], I32)
        hi_int = sb("hi_int", [P, CHUNKS], I32)
        dst_f = sb("dst_f", [P, CHUNKS])
        lo = sb("lo", [P, CHUNKS], BF16)
        hi = sb("hi", [P, CHUNKS], BF16)
        first = sb("first", [1, 1])
        squared = sb("squared", [P, GROUP, P], BF16)
        apart = sb("apart", [P, 2, GROUP, P], BF16)
        iota = sb("iota_bf16", [P, P], BF16)
        base_f = sb("base_f", [1, CHUNKS])
        ones = sb("ones", [1, P])
        iota_int = sb("iota_int", [P, P], I32)
        iota_p_int = sb("iota_p_int", [P, 1], I32)
        zeros = sb("zeros", [P, P], BF16)
        lo_hot = sb("lo_hot", [P, 2, GROUP, P], BF16)
        hi_hot = sb("hi_hot", [P, 2, GROUP, TILES], BF16)
        counts = sb("counts", [TILES, P])
        root = sb("root", [P, 2, TILES])
        seen = sb("seen", [P, TILES])
        base_ps = core.ps(ctx, "base_ps", [P, 2, 512])
        hist_ps = core.ps(ctx, "hist_ps", [P, 512])
        deg_ps = core.ps(ctx, "deg_ps", [P, 512])

        loaded = core.sem("setup_loaded")
        x_loaded = core.sem("setup_x_loaded")
        x_zeroed = core.sem("setup_x_zeroed")
        made = core.sem("setup_constants")
        ident_zeroed = core.sem("setup_ident_zeroed")
        step = core.sem("setup_vector_step")
        split = core.sem("setup_hi_lo")
        base_ready = core.sem("setup_base_ready")
        base_spread = core.sem("setup_base_spread")
        lo_ready = [core.sem(f"setup_lo_hot{s}") for s in range(2)]
        apart_ready = core.sem("setup_apart")
        apart_used = core.sem("setup_apart_used")
        hi_ready = core.sem("setup_hi_hot")
        counted = core.sem("setup_counted")
        counts_ready = core.sem("setup_counts")
        deg_ready = core.sem("setup_deg")
        root_in = core.sem("setup_root_in")
        rooted = core.sem("setup_rooted")
        half = CHUNKS // 2

        block = ctx.enter_context(nc.Block())

        @block.sync
        def _(sp):
            sp.dma_start(dst_int[:], dst_cols).then_inc(loaded, 16)
            sp.dma_start(k.base_row[:], base_row).then_inc(loaded, 16)
            sp.dma_start(k.src[:, 0:CHUNKS], src_cols).then_inc(loaded, 16)
            sp.wait_ge(x_zeroed, 1)
            sp.dma_start(k.x[:, 0:FULL_TILES, :],
                         x[0:FULL_TILES * P, :].rearrange("(t p) f -> p t f", p=P)).then_inc(x_loaded, 16)
            sp.dma_start(k.x[0:TAIL, FULL_TILES, :], x[FULL_TILES * P:N_NODES, :]).then_inc(x_loaded, 16)
            sp.wait_ge(x_loaded, 32)

        @block.gpsimd
        def _(pool):
            nc.gpsimd.iota(iota_int[:], pattern=[[1, P]], base=0, channel_multiplier=0).then_inc(made, 1)
            nc.gpsimd.iota(iota_p_int[:], pattern=[[0, 1]], base=0, channel_multiplier=1).then_inc(made, 1)
            nc.gpsimd.memset(k.ident[:], 0.0).then_inc(ident_zeroed, 1)
            nc.gpsimd.memset(k.src[:, CHUNKS:], 0)
            nc.gpsimd.memset(k.x[:, FULL_TILES:TILES, :], 0.0).then_inc(x_zeroed, 1)
            pool.wait_ge(ident_zeroed, 1)
            nc.gpsimd.affine_select(out=k.ident[:], in_=k.ident[:], compare_op=ALU.not_equal, fill=1.0,
                                    base=0, pattern=[[-1, P]], channel_multiplier=1).then_inc(made, 1)
            pool.wait_ge(split, 3)
            with pool.Fori(0, GROUPS // 4) as i:
                for j in range(2):
                    first_chunk = i * (4 * GROUP) + (2 * j + 1) * GROUP
                    pool.wait_ge(apart_used, i * 2 + (j + 1))
                    nc.gpsimd.tensor_tensor(apart[:, j, :, :], wide(lo[:, bass.ds(first_chunk, GROUP)], P),
                                            along(iota[:], GROUP), ALU.subtract).then_inc(apart_ready, 1)

        @block.vector
        def _(dve):
            dve.wait_ge(made, 3)
            nc.vector.tensor_copy(k.iota[:], iota_int[:])
            nc.vector.tensor_copy(iota[:], iota_int[:]).then_inc(step, 1)
            nc.vector.tensor_copy(k.iota_p[:], iota_p_int[:]).then_inc(step, 1)
            nc.vector.memset(ones[:], 1.0).then_inc(step, 1)
            nc.vector.memset(zeros[:], 0.0).then_inc(step, 1)
            dve.wait_ge(loaded, 48)
            nc.vector.tensor_copy(base_f[:], k.base_row[0:1, :]).then_inc(base_ready, 1)
            nc.vector.tensor_scalar(hi_int[:], dst_int[:], 7, None, ALU.logical_shift_right).then_inc(step, 1)
            nc.vector.tensor_scalar(lo_int[:], dst_int[:], P - 1, None, ALU.bitwise_and).then_inc(step, 1)
            nc.vector.tensor_copy(dst_f[:], dst_int[:]).then_inc(step, 1)
            nc.vector.memset(k.local[:, CHUNKS:], 0.0).then_inc(step, 1)
            dve.wait_ge(step, 8)
            nc.vector.tensor_copy(hi[:], hi_int[:]).then_inc(split, 1)
            nc.vector.tensor_copy(lo[:], lo_int[:]).then_inc(split, 1)
            dve.wait_ge(base_spread, 1)
            nc.vector.tensor_tensor(k.local[:, 0:CHUNKS].rearrange("p (a b) -> p a b", a=2),
                                    dst_f[:].rearrange("p (a b) -> p a b", a=2),
                                    base_ps[:, :, 0:half], ALU.subtract).then_inc(split, 1)
            dve.wait_ge(split, 3)
            with dve.Fori(0, GROUPS // 4) as i:
                for j in range(4):
                    g, s = i * 4 + j, j % 2
                    dve.wait_ge(counted, g + 1)
                    if s == 0:
                        nc.vector.tensor_tensor(lo_hot[:, s, :, :], wide(lo[:, bass.ds(g * GROUP, GROUP)], P),
                                                along(iota[:], GROUP), ALU.is_equal).then_inc(lo_ready[0], 1)
                    nc.vector.tensor_tensor(hi_hot[:, s, :, :], wide(hi[:, bass.ds(g * GROUP, GROUP)], TILES),
                                            along(iota[:, 0:TILES], GROUP), ALU.is_equal).then_inc(hi_ready, 1)
            dve.wait_ge(counted, GROUPS + 2)
            nc.vector.tensor_copy(counts[:], hist_ps[0:TILES, 0:P]).then_inc(counts_ready, 1)
            dve.wait_ge(deg_ready, 1)
            nc.vector.tensor_scalar(root[:, 0, :], deg_ps[:, 0:TILES], 1.0, None, ALU.add).then_inc(root_in, 1)
            nc.vector.tensor_scalar(root[:, 1, :], deg_ps[:, 0:TILES], 1.0, None, ALU.max).then_inc(root_in, 1)
            nc.vector.tensor_scalar(seen[:], deg_ps[:, 0:TILES], 0.0, None, ALU.is_gt).then_inc(root_in, 1)
            dve.wait_ge(rooted, 1)
            nc.vector.reciprocal(k.dinv[:], root[:, 0, :]).then_inc(root_in, 1)
            nc.vector.reciprocal(root[:, 1, :], root[:, 1, :]).then_inc(root_in, 1)
            dve.wait_ge(root_in, 5)
            nc.vector.tensor_tensor(k.deg_inv[:], root[:, 1, :], seen[:], ALU.mult).then_inc(root_in, 1)

        @block.tensor
        def _(pe):
            pe.wait_ge(base_ready, 1)
            pe.wait_ge(step, 4)
            for h in range(2):
                mm = nc.tensor.matmul(base_ps[:, h, 0:half], ones[:], base_f[:, h * half:(h + 1) * half],
                                      start=True, stop=True)
            mm.then_inc(base_spread, 1)
            nc.tensor.matmul(hist_ps[0:TILES, 0:P], zeros[:, 0:TILES], zeros[:], start=True, stop=False,
                             skip_group_check=True).then_inc(counted, 2)
            with pe.Fori(0, GROUPS // 4) as i:
                for j in range(4):
                    s = j % 2
                    pe.wait_ge(lo_ready[s], i * 2 + (j // 2 + s + 1))
                    pe.wait_ge(hi_ready, i * 4 + (j + 1))
                    for c in range(GROUP):
                        mm = nc.tensor.matmul(hist_ps[0:TILES, 0:P], hi_hot[:, s, c, :], lo_hot[:, s, c, :],
                                              start=False, stop=False, skip_group_check=True)
                    mm.then_inc(counted, 1)
            pe.wait_ge(counts_ready, 1)
            pe.wait_ge(made, 3)
            nc.tensor.transpose(deg_ps[:, 0:TILES], counts[:], k.ident[0:TILES, 0:TILES]).then_inc(deg_ready, 1)

        @block.scalar
        def _(act):
            act.sem_inc(apart_used, 2)
            act.sem_inc(lo_ready[1], 1)
            act.wait_ge(step, 4)
            nc.scalar.activation(first[:], ones[0:1, 0:1], ACT.Square)
            with act.Fori(0, GROUPS // 4) as i:
                for j in range(2):
                    act.wait_ge(apart_ready, i * 2 + (j + 1))
                    act.wait_ge(lo_ready[1], i * 2 + (j + 1))
                    nc.scalar.activation(squared[:], apart[:, j, :, :], ACT.Square).then_inc(apart_used, 1)
                    act.wait_ge(apart_used, i * 2 + (j + 3))
                    act.wait_ge(counted, i * 4 + (2 * j + 2))
                    nc.scalar.activation(lo_hot[:, 1, :, :], squared[:], ACT.Relu, bias=1.0, scale=-1.0
                                         ).then_inc(lo_ready[1], 1)
            act.wait_ge(root_in, 3)
            nc.scalar.activation(root[:], root[:], ACT.Sqrt).then_inc(rooted, 1)


def sum_over_edges(core, k, name, table, width, acc, kinds):
    nc = core.nc
    with ExitStack() as ctx:
        rows = core.sb(ctx, f"{name}_rows", [P, RING, GROUP, width])
        index = core.sb(ctx, f"{name}_index", [P, RING, GROUP], I32)
        hot = core.sb(ctx, f"{name}_hot", [P, 2, HALF, P])
        sums = [core.ps(ctx, f"{name}_sums{h}", [P, kinds, HALF, P]) for h in range(2)]

        staged = core.sem(f"{name}_index_staged")
        landing, before = k.landing, k.landed
        k.landed += ROUNDS * 16 * GROUP
        hot_ready = core.sem(f"{name}_hot_ready")
        summed = core.sem(f"{name}_summed")
        added = core.sem(f"{name}_added")
        FREE, EMPTY = 2 * RING, 2 * HALF

        block = ctx.enter_context(nc.Block())

        @block.scalar
        def _(act):
            with act.Fori(0, ROUNDS) as i:
                for r in range(RING):
                    act.wait_ge(summed, i * 2 * RING + (2 * r + 2))
                    nc.scalar.copy(index[:, r, :], k.src[:, bass.ds(i * RING * GROUP + r * GROUP, GROUP)]
                                   ).then_inc(staged, 1)

        @block.gpsimd
        def _(pool):
            with pool.Fori(0, ROUNDS) as i:
                for r in range(RING):
                    pool.wait_ge(staged, i * RING + (r + 1))
                    core.hold(pool)
                    for c in range(GROUP):
                        nc.gpsimd.indirect_dma_start(
                            out=rows[:, r, c, :], out_offset=None, in_=table,
                            in_offset=bass.IndirectOffsetOnAxis(ap=index[:, r, c:c + 1], axis=0),
                        ).then_inc(landing[r], 16)

        @block.tensor
        def _(pe):
            pe.sem_inc(summed, FREE)
            with pe.Fori(0, ROUNDS) as i:
                for r in range(RING):
                    pe.wait_ge(landing[r], i * 16 * GROUP + (before + 16 * GROUP))
                    for h in range(2):
                        pe.wait_ge(hot_ready, i * 2 * RING + (2 * r + h + 1))
                        pe.wait_ge(added, i * 2 * RING * HALF + ((2 * r + h) * HALF + HALF))
                        for c in range(HALF):
                            row = rows[:, r, HALF * h + c, :]
                            mm = nc.tensor.matmul(sums[h][:, 0, c, :], row[:, 0:D], hot[:, h, c, :],
                                                  start=True, stop=True)
                            if kinds == 2:
                                mm = nc.tensor.matmul(sums[h][:, 1, c, :],
                                                      row[:, D:D + 1].to_broadcast([P, P]),
                                                      hot[:, h, c, :], start=True, stop=True)
                        mm.then_inc(summed, 1)

        @block.vector
        def _(dve):
            base = [dve.alloc_register(f"{name}_base{c}") for c in range(GROUP)]

            def make_hot(first, h):
                nc.vector.tensor_tensor(hot[:, h, :, :], wide(k.local[:, bass.ds(first, HALF)], P),
                                        along(k.iota[:], HALF), ALU.is_equal).then_inc(hot_ready, 1)

            nc.vector.memset(acc, 0.0).then_inc(added, EMPTY)
            make_hot(0, 0)
            with dve.Fori(0, ROUNDS) as i:
                for r in range(RING):
                    first_node = load_bases(dve, base, k.base_row, i * RING * GROUP + r * GROUP)
                    for h in range(2):
                        n = 2 * r + h
                        dve.wait_ge(summed, i * 2 * RING + (FREE + n))
                        make_hot(i * RING * GROUP + (n + 1) * HALF, 1 - h)
                        dve.wait_ge(summed, i * 2 * RING + (FREE + n + 1))
                        for c in range(HALF):
                            dve.wait_ge(added, i * 2 * RING * HALF + (EMPTY + n * HALF + c))
                            at = first_node[HALF * h + c]
                            window = acc[:, :, bass.ds(at, P)]
                            nc.vector.tensor_tensor(window, window, sums[h][:, :, c, :], ALU.add
                                                    ).then_inc(added, 1)
            dve.wait_ge(added, EMPTY + CHUNKS)


LANES = range(2)


def in_lanes(eng, stages, steps):
    lag = stages // 2

    def pair(p, earlier, later):
        for stage in range(stages):
            if stage in steps:
                steps[stage](p * 2, p, 0)
            if earlier and stage < lag and stage + stages - lag in steps:
                steps[stage + stages - lag](p * 2 - 1, p - 1, 1)
            if later and stage >= lag and stage - lag in steps:
                steps[stage - lag](p * 2 + 1, p, 1)

    pair(0, False, True)
    with eng.Fori(1, QUADS // 2) as p:
        pair(p, True, True)
    pair(QUADS // 2, True, False)


class Steps:

    def __init__(self, core, name, steps):
        self.sem, self.steps = core.sem(name), steps

    def start(self, eng):
        eng.sem_inc(self.sem, self.steps)

    def wait(self, eng, i, step):
        eng.wait_ge(self.sem, i * self.steps + (self.steps + step))

    def wait_before(self, eng, i, step):
        eng.wait_ge(self.sem, i * self.steps + step)


def rows_of(dram, i):
    return dram[bass.ds(i * (QUAD * P), QUAD * P), :].rearrange("(t p) f -> p t f", p=P)


def propagate_nodes(core, k, acc, table):
    nc = core.nc
    with ExitStack() as ctx:
        features = core.sb(ctx, "hop_features", [P, QUAD * P])
        weighted = core.sb(ctx, "hop_weighted", [P, QUAD, D])
        c_acc = core.sb(ctx, "hop_c_acc", [P, TILES])
        c_self = core.sb(ctx, "hop_c_self", [P, TILES])
        nodes = core.ps(ctx, "hop_nodes", [P, QUAD, D])
        copied = Steps(core, "hop_copied", 1)
        turned = Steps(core, "hop_turned", 1)
        mixed = Steps(core, "hop_mixed", 3)
        stored = core.sem("hop_stored")
        coeff = core.sem("hop_coefficients")
        block = ctx.enter_context(nc.Block())

        @block.scalar
        def _(act):
            copied.start(act)
            with act.Fori(0, QUADS) as i:
                turned.wait_before(act, i, 1)
                nc.scalar.copy(features[:], acc[:, 0, bass.ds(i * (QUAD * P), QUAD * P)]).then_inc(copied.sem, 1)

        @block.tensor
        def _(pe):
            turned.start(pe)
            with pe.Fori(0, QUADS) as i:
                copied.wait(pe, i, 1)
                mixed.wait_before(pe, i, 1)
                for t in range(QUAD):
                    mm = nc.tensor.transpose(nodes[:, t, :], features[:, t * P:(t + 1) * P], k.ident[:])
                mm.then_inc(turned.sem, 1)

        @block.vector
        def _(dve):
            mixed.start(dve)
            nc.vector.scalar_tensor_tensor(out=c_acc[:], in0=k.dinv[:], scalar=0.5, in1=k.dinv[:],
                                           op0=ALU.mult, op1=ALU.mult).then_inc(coeff, 1)
            dve.wait_ge(coeff, 1)
            nc.vector.tensor_scalar(c_self[:], c_acc[:], 0.5, None, ALU.add).then_inc(coeff, 1)
            dve.wait_ge(coeff, 2)
            with dve.Fori(0, QUADS) as i:
                scaled = k.scaled[:, bass.ds(i * QUAD, QUAD), :]
                turned.wait(dve, i, 1)
                nc.vector.tensor_tensor(weighted[:], nodes[:], wide(c_acc[:, bass.ds(i * QUAD, QUAD)], D),
                                        ALU.mult).then_inc(mixed.sem, 1)
                nc.vector.tensor_tensor(scaled, scaled, wide(c_self[:, bass.ds(i * QUAD, QUAD)], D),
                                        ALU.mult).then_inc(mixed.sem, 1)
                mixed.wait(dve, i, 2)
                nc.vector.tensor_tensor(scaled, scaled, weighted[:], ALU.add).then_inc(mixed.sem, 1)
                mixed.wait(dve, i, 3)

        @block.sync
        def _(sp):
            with sp.Fori(0, QUADS) as i:
                mixed.wait(sp, i, 3)
                sp.dma_start(rows_of(table, i), k.scaled[:, bass.ds(i * QUAD, QUAD), :]).then_inc(stored, 16)
            sp.wait_ge(stored, 16 * QUADS)


class Norm:

    def __init__(self, core, ctx, name, z):
        self.core, self.nc, self.z = core, core.nc, z
        self.stats = core.sb(ctx, f"{name}_stats", [P, QUAD, 6])
        self.mean_var = core.sb(ctx, f"{name}_mean_var", [P, QUAD, 2])
        self.deviation = core.sb(ctx, f"{name}_deviation", [P, QUAD])
        self.eps = core.sb(ctx, f"{name}_eps", [P, 1])

    def take_statistics(self, dve, n, vector, v):
        nc = self.nc
        vector.wait(dve, n, v)
        for t in range(QUAD):
            last = nc.vector.bn_stats(self.stats[:, t, :], self.z[:, t, :])
        last.then_inc(vector.sem, 1)
        vector.wait(dve, n, v + 1)
        self.core.hold(dve)
        for t in range(QUAD):
            last = nc.vector.bn_aggr(self.mean_var[:, t, :], self.stats[:, t, :])
        last.then_inc(vector.sem, 1)

    def root(self, act, n, vector, v, scalar):
        vector.wait(act, n, v + 2)
        self.nc.scalar.activation(self.deviation[:], self.mean_var[:, :, 1], ACT.Sqrt,
                                  bias=self.eps[:]).then_inc(scalar.sem, 1)

    def rescale(self, dve, n, vector, v, scalar, s):
        nc = self.nc
        scalar.wait(dve, n, s)
        nc.vector.reciprocal(self.deviation[:], self.deviation[:]).then_inc(vector.sem, 1)
        vector.wait(dve, n, v + 3)
        for t in range(QUAD):
            last = nc.vector.tensor_scalar(self.z[:, t, :], self.z[:, t, :], self.mean_var[:, t, 0:1],
                                           self.deviation[:, t:t + 1], ALU.subtract, ALU.mult)
        last.then_inc(vector.sem, 1)


def leave_l0(core, k, ins, acc, x_out, table, dst_table):
    nc = core.nc
    WT = D + 2 * HEADS
    with ExitStack() as ctx:
        def sb(name, shape, dt=F32):
            return core.sb(ctx, f"l0_{name}", shape, dt)

        def of_lanes(name, shape):
            return [sb(f"{name}{lane}", shape) for lane in LANES]

        def ps_of_lanes(name, shape):
            return [core.ps(ctx, f"l0_{name}{lane}", shape) for lane in LANES]

        w1, w2t, w12 = sb("w1", [P, D]), sb("w2t", [P, D]), sb("w12", [P, D])
        b1, b2, b12 = sb("b1", [P, 1]), sb("b2", [1, D]), sb("b12", [1, D])
        ones = sb("ones", [1, P])
        w_heads = sb("w_heads", [P, WT])
        att = sb("att", [P, HEADS, 2, HC])
        product = sb("product", [P, HEADS, HC])
        half_dinv = sb("half_dinv", [P, TILES])
        features = of_lanes("features", [P, QUAD * P])
        mix = of_lanes("mix", [P, QUAD, D])
        relu_t = of_lanes("relu_t", [P, QUAD * P])
        z = of_lanes("z", [P, QUAD, D])
        z_t = of_lanes("z_t", [P, QUAD * P])
        h = of_lanes("h", [P, QUAD, WT])
        norm = [Norm(core, ctx, f"l0_{lane}", z[lane]) for lane in LANES]
        nodes = ps_of_lanes("nodes", [P, QUAD, D])
        out_ps = nodes
        turned_ps = ps_of_lanes("turned", [P, QUAD, D])
        h_ps = ps_of_lanes("heads_ps", [P, 2, 512])
        w_ps = h_ps[1][:, 0, :]
        loaded = core.sem("l0_loaded")
        ready = core.sem("l0_weights_step")
        multiplied = core.sem("l0_weights_product")
        A = [Steps(core, f"l0_scalar{lane}", 5) for lane in LANES]
        T = [Steps(core, f"l0_tensor{lane}", 5) for lane in LANES]
        V = [Steps(core, f"l0_vector{lane}", 8) for lane in LANES]
        stored = [Steps(core, f"l0_stored{lane}", 48) for lane in LANES]
        READY = 10
        STAGES = 14
        block = ctx.enter_context(nc.Block())

        @block.sync
        def _(sp):
            sp.dma_start(w1[:], ins["L0_gnn_w1"]).then_inc(loaded, 16)
            sp.dma_start(w2t[:], ins["w2_t"]).then_inc(loaded, 16)
            sp.dma_start(b1[:], ins["L0_gnn_b1"].rearrange("(p a) -> p a", a=1)).then_inc(loaded, 16)
            sp.dma_start(b2[:], ins["L0_gnn_b2"].rearrange("(a p) -> a p", a=1)).then_inc(loaded, 16)
            sp.dma_start(w_heads[:, 0:D], ins["L1_gnn_weight"]).then_inc(loaded, 16)
            sp.dma_start(att[:].rearrange("p h s c -> p (h s c)"),
                         ins["L1_gnn_att"].rearrange("a h c -> a (h c)").to_broadcast([P, 2 * D])).then_inc(loaded, 16)

            def store_x(i, n, lane):
                V[lane].wait(sp, n, 8)
                sp.dma_start(rows_of(x_out, i), z[lane][:]).then_inc(stored[lane].sem, 16)

            def store_tables(i, n, lane):
                A[lane].wait(sp, n, 5)
                sp.dma_start(rows_of(table, i), h[lane][:, :, 0:D + HEADS]).then_inc(stored[lane].sem, 16)
                sp.dma_start(rows_of(dst_table, i), h[lane][:, :, D + HEADS:WT]).then_inc(stored[lane].sem, 16)

            for lane in LANES:
                stored[lane].start(sp)
            in_lanes(sp, STAGES, {10: store_x, 13: store_tables})
            for lane in LANES:
                stored[lane].wait_before(sp, (QUADS + 1 - lane) // 2, 48)

        @block.vector
        def _(dve):
            for lane in LANES:
                V[lane].start(dve)
                nc.vector.memset(norm[lane].eps[:], EPS)
            nc.vector.memset(ones[:], 1.0).then_inc(ready, 2)
            nc.vector.tensor_scalar(half_dinv[:], k.dinv[:], 0.5, None, ALU.mult).then_inc(ready, 1)
            dve.wait_ge(loaded, 96)
            heads = w_heads[:, 0:D].rearrange("p (h c) -> p h c", h=HEADS)
            for s in range(2):
                nc.vector.tensor_tensor(product[:], heads, att[:, :, s, :], ALU.mult).then_inc(ready, 1)
                dve.wait_ge(ready, 4 + 2 * s)
                nc.vector.tensor_reduce(w_heads[:, D + HEADS * s:D + HEADS * (s + 1)], product[:], AX_X,
                                        ALU.add).then_inc(ready, 1)
                dve.wait_ge(ready, 5 + 2 * s)
            dve.wait_ge(multiplied, 1)
            nc.vector.tensor_copy(w12[:], w_ps[:, 0:D]).then_inc(ready, 1)
            nc.vector.tensor_tensor(b12[:], w_ps[0:1, D:2 * D], b2[:], ALU.add).then_inc(ready, 1)
            dve.wait_ge(ready, READY - 1)
            nc.vector.memset(mix[0][:, 0, 0:1], 0.0).then_inc(ready, 1)
            dve.wait_ge(ready, READY)

            def mix_hops(i, n, lane):
                tiles = bass.ds(i * QUAD, QUAD)
                mixed = mix[lane][:]
                T[lane].wait(dve, n, 1)
                nc.vector.tensor_tensor(mixed, nodes[lane][:], k.scaled[:, tiles, :], ALU.add
                                        ).then_inc(V[lane].sem, 1)
                V[lane].wait(dve, n, 1)
                nc.vector.tensor_tensor(mixed, mixed, wide(half_dinv[:, tiles], D), ALU.mult
                                        ).then_inc(V[lane].sem, 1)
                V[lane].wait(dve, n, 2)
                nc.vector.scalar_tensor_tensor(out=mixed, in0=k.x[:, tiles, :], scalar=0.5, in1=mixed,
                                               op0=ALU.mult, op1=ALU.add).then_inc(V[lane].sem, 1)

            def add_x(i, n, lane):
                T[lane].wait(dve, n, 3)
                stored[lane].wait_before(dve, n, 48)
                nc.vector.tensor_tensor(z[lane][:], out_ps[lane][:], k.x[:, bass.ds(i * QUAD, QUAD), :], ALU.add
                                        ).then_inc(V[lane].sem, 1)
                norm[lane].take_statistics(dve, n, V[lane], 4)

            def rescale(i, n, lane):
                norm[lane].rescale(dve, n, V[lane], 4, A[lane], 3)

            in_lanes(dve, STAGES, {2: mix_hops, 6: add_x, 8: rescale})

        @block.tensor
        def _(pe):
            for lane in LANES:
                T[lane].start(pe)
            pe.wait_ge(loaded, 96)
            nc.tensor.matmul(w_ps[:, 0:D], w1[:], w2t[:], start=True, stop=True)
            nc.tensor.matmul(w_ps[0:1, D:2 * D], b1[:], w2t[:], start=True, stop=True).then_inc(multiplied, 1)
            pe.wait_ge(ready, READY)

            def to_nodes(i, n, lane):
                A[lane].wait(pe, n, 1)
                V[lane].wait_before(pe, n, 4)
                for t in range(QUAD):
                    mm = nc.tensor.transpose(nodes[lane][:, t, :], features[lane][:, t * P:(t + 1) * P], k.ident[:])
                mm.then_inc(T[lane].sem, 1)

            def turn_mix(i, n, lane):
                V[lane].wait(pe, n, 3)
                for t in range(QUAD):
                    mm = nc.tensor.transpose(turned_ps[lane][:, t, :], mix[lane][:, t, :], k.ident[:])
                mm.then_inc(T[lane].sem, 1)

            def linear(i, n, lane):
                A[lane].wait(pe, n, 2)
                for t in range(QUAD):
                    nc.tensor.matmul(out_ps[lane][:, t, :], relu_t[lane][:, t * P:(t + 1) * P], w12[:],
                                     start=True, stop=False)
                    mm = nc.tensor.matmul(out_ps[lane][:, t, :], ones[:], b12[:], start=False, stop=True)
                mm.then_inc(T[lane].sem, 1)

            def turn_x(i, n, lane):
                V[lane].wait(pe, n, 8)
                for t in range(QUAD):
                    mm = nc.tensor.transpose(turned_ps[lane][:, t, :], z[lane][:, t, :], k.ident[:])
                mm.then_inc(T[lane].sem, 1)

            def project(i, n, lane):
                A[lane].wait(pe, n, 4)
                for t in range(QUAD):
                    mm = nc.tensor.matmul(h_ps[lane][:, t // 2, (t % 2) * WT:(t % 2 + 1) * WT],
                                          z_t[lane][:, t * P:(t + 1) * P], w_heads[:], start=True, stop=True)
                mm.then_inc(T[lane].sem, 1)

            in_lanes(pe, STAGES, {1: to_nodes, 3: turn_mix, 5: linear, 9: turn_x, 11: project})

        @block.scalar
        def _(act):
            for lane in LANES:
                A[lane].start(act)
            act.wait_ge(ready, READY)

            def fetch(i, n, lane):
                T[lane].wait_before(act, n, 1)
                nc.scalar.copy(features[lane][:], acc[:, 0, bass.ds(i * (QUAD * P), QUAD * P)]
                               ).then_inc(A[lane].sem, 1)

            def relu(i, n, lane):
                T[lane].wait(act, n, 2)
                nc.scalar.activation(relu_t[lane][:].rearrange("p (t n) -> p t n", t=QUAD), turned_ps[lane][:],
                                     ACT.Relu).then_inc(A[lane].sem, 1)

            def root(i, n, lane):
                norm[lane].root(act, n, V[lane], 4, A[lane])

            def take_x(i, n, lane):
                T[lane].wait(act, n, 4)
                nc.scalar.copy(z_t[lane][:].rearrange("p (t n) -> p t n", t=QUAD), turned_ps[lane][:]
                               ).then_inc(A[lane].sem, 1)

            def take_h(i, n, lane):
                T[lane].wait(act, n, 5)
                stored[lane].wait_before(act, n, 48)
                nc.scalar.copy(h[lane][:].rearrange("p (a b) f -> p a (b f)", a=2), h_ps[lane][:, :, 0:2 * WT]
                               ).then_inc(A[lane].sem, 1)

            in_lanes(act, STAGES, {0: fetch, 4: relu, 7: root, 10: take_x, 12: take_h})




def mark_segments(core, k, dst_line):
    nc = core.nc
    with ExitStack() as ctx:
        def sb(name, shape, dt=F32):
            return core.sb(ctx, f"mark_{name}", shape, dt)

        names = [sb(n, [ROWS, SUPERS, P], I32) for n in ("before", "here", "after")]
        values = [sb(n, [ROWS, SUPERS, P]) for n in ("before_f", "here_f", "after_f")]
        local = sb("local", [ROWS, SUPERS, P], BF16)
        row_keeps = sb("row_keeps", [ROWS, 2, SUPERS])
        level_ps = core.ps(ctx, "mark_level", [HEADS, 2, SUPERS, P])
        loaded, step, turned, stored = (core.sem(f"mark_{n}") for n in ("loaded", "step", "turned", "stored"))
        heads_cut = core.sem("mark_heads_cut")
        block = ctx.enter_context(nc.Block())

        @block.sync
        def _(sp):
            for n in range(3):
                sp.dma_start(names[n][:], dst_line[n:n + E_PAD].rearrange("(s p e) -> p s e", s=SUPERS, p=ROWS)
                             ).then_inc(loaded, 16)
            sp.wait_ge(step, 4)
            sp.dma_start(k.local_rows.rearrange("(s p) e -> p s e", p=ROWS), local[:]).then_inc(stored, 16)
            sp.wait_ge(stored, 16)

        @block.vector
        def _(dve):
            dve.wait_ge(loaded, 48)
            for n in range(3):
                nc.vector.tensor_copy(values[n][:], names[n][:]).then_inc(step, 1)
            dve.wait_ge(step, 3)
            before, here, after = (v[:] for v in values)
            first = values[1][:, :, 0:1].to_broadcast([ROWS, SUPERS, P])
            nc.vector.tensor_tensor(local[:], here, first, ALU.subtract).then_inc(step, 1)
            nc.vector.tensor_tensor(k.goes_on[:], here, before, ALU.is_equal).then_inc(step, 1)
            nc.vector.tensor_tensor(k.stays[:], here, after, ALU.is_equal).then_inc(step, 1)
            nc.vector.tensor_tensor(k.ends[:], here, after, ALU.not_equal).then_inc(step, 1)
            dve.wait_ge(step, 7)
            nc.vector.tensor_scalar(k.reset[:], k.goes_on[:], -1.0, BIG, ALU.add, ALU.mult).then_inc(step, 1)
            nc.vector.tensor_reduce(row_keeps[:, 0, :], k.goes_on[:], AX_X, ALU.min).then_inc(step, 1)
            nc.vector.tensor_reduce(row_keeps[:, 1, :], k.stays[:], AX_X, ALU.min).then_inc(step, 1)
            nc.vector.memset(k.heads_on[:], 1.0).then_inc(step, 1)
            dve.wait_ge(turned, 1)
            nc.vector.tensor_copy(k.row_goes_on[:], level_ps[:, 0, :, 0:ROWS]).then_inc(step, 1)
            nc.vector.tensor_copy(k.row_stays[:], level_ps[:, 1, :, 0:ROWS]).then_inc(step, 1)
            dve.wait_ge(step, 13)
            nc.vector.tensor_scalar(k.row_reset[:], k.row_goes_on[:], -1.0, BIG, ALU.add, ALU.mult
                                    ).then_inc(step, 1)

        @block.gpsimd
        def _(pool):
            pool.wait_ge(step, 11)
            nc.gpsimd.affine_select(out=k.heads_on[:], in_=k.heads_on[:], compare_op=ALU.is_ge, fill=0.0,
                                    base=0, pattern=[[1, D]], channel_multiplier=-HC).then_inc(heads_cut, 1)
            pool.wait_ge(heads_cut, 1)
            nc.gpsimd.affine_select(out=k.heads_on[:], in_=k.heads_on[:], compare_op=ALU.is_ge, fill=0.0,
                                    base=HC - 1, pattern=[[-1, D]], channel_multiplier=HC).then_inc(heads_cut, 1)

        @block.tensor
        def _(pe):
            pe.wait_ge(step, 10)
            for kind in range(2):
                for s in range(SUPERS):
                    keeps = row_keeps[:, kind, s:s + 1].to_broadcast([ROWS, HEADS])
                    mm = nc.tensor.transpose(level_ps[:, kind, s, 0:ROWS], keeps, k.ident[0:ROWS, 0:ROWS])
            mm.then_inc(turned, 1)


class SegmentSoftmax:

    VECTOR_STEPS = 33
    TENSOR_STEPS = 10
    SCALAR_STEPS = 3

    def __init__(self, core, k, ctx, name, scale):
        def sb(n, shape, dt=F32):
            return core.sb(ctx, f"{name}_{n}", shape, dt)

        self.core, self.nc, self.k, self.scale = core, core.nc, k, scale
        self.logits = sb("logits", [P, ROWS, HEADS])
        self.lg = sb("row_logits", [ROWS, HEADS, P])
        self.run = sb("running", [ROWS, HEADS, P])
        self.at_end = sb("at_end", [ROWS, HEADS, P])
        self.whole = sb("whole", [ROWS, HEADS, P])
        self.carried = sb("carried", [ROWS, HEADS])
        self.row_max = sb("row_max", [HEADS, ROWS + 1])
        self.row_sum = sb("row_sum", [HEADS, ROWS + 1])
        self.row_max_back = sb("row_max_back", [HEADS, ROWS + 1])
        self.row_sum_back = sb("row_sum_back", [HEADS, ROWS + 1])
        self.stays = sb("stays", [ROWS, P], BF16)
        self.row_stays = sb("row_stays", [HEADS, ROWS])
        self.copied = core.sem(f"{name}_softmax_copied")
        self.shift = sb("shift", [HEADS, 1])
        self.factor = sb("factor", [HEADS, 1])
        self.weights = sb("weights", [P, HEADS, ROWS])
        self.rescale = sb("rescale", [P, 1])
        self.big_ps = core.ps(ctx, f"{name}_softmax_rows", [P, 512])
        self.small_ps = core.ps(ctx, f"{name}_softmax_level", [P, 512])
        self.V = Steps(core, f"{name}_softmax_vector", self.VECTOR_STEPS)
        self.T = Steps(core, f"{name}_softmax_tensor", self.TENSOR_STEPS)
        self.A = Steps(core, f"{name}_softmax_scalar", self.SCALAR_STEPS)
        self.emptied = core.sem(f"{name}_softmax_emptied")
        self.rows_ps = self.big_ps[0:ROWS, :].rearrange("p (h e) -> p h e", h=HEADS)
        self.level_ps = self.small_ps[0:HEADS, 0:ROWS]
        self.back_ps = self.small_ps[0:ROWS, P:P + HEADS]
        self.rescale_ps = self.small_ps[:, 2 * P:2 * P + 1]
        self.weights_ps = self.big_ps[:, 0:HEADS * ROWS].rearrange("p (h j) -> p h j", h=HEADS)

    def start_vector(self, dve):
        self.V.start(dve)
        self.nc.vector.memset(self.row_max[:, ROWS:], -BIG).then_inc(self.emptied, 1)
        self.nc.vector.memset(self.row_sum[:, ROWS:], 0.0).then_inc(self.emptied, 1)
        dve.wait_ge(self.emptied, 2)

    def vector(self, dve, s):
        nc, k, V, T, A = self.nc, self.k, self.V, self.T, self.A
        reset, goes_on, ends, row_reset, row_goes_on = (
            m[:, bass.ds(s, 1), :].rearrange("p a e -> p (a e)")
            for m in (k.reset, k.goes_on, k.ends, k.row_reset, k.row_goes_on))

        def scans(out, keep, x, initial, op0, op1, back=False):
            for h in range(HEADS):
                o, a, b = out[:, h, :], keep, x[:, h, :]
                if back:
                    o, a, b = o[:, ::-1], a[:, ::-1], b[:, ::-1]
                first = initial if isinstance(initial, float) else initial[:, h:h + 1]
                last = nc.vector.tensor_tensor_scan(out=o, data0=a, data1=b, initial=first, op0=op0, op1=op1)
            last.then_inc(V.sem, 1)

        def both_ways(x, level, level_back, keep, row_keep, empty, op0, op1, v, t):
            scans(self.run, keep, x, empty, op0, op1)
            T.wait(dve, s, t + 1)
            V.wait(dve, s, v)
            nc.vector.tensor_tensor_scan(out=level[:, 1:ROWS + 1], data0=row_keep, data1=self.level_ps,
                                         initial=level[:, 0:1], op0=op0, op1=op1).then_inc(V.sem, 1)
            T.wait(dve, s, t + 2)
            nc.vector.tensor_copy(self.carried[:], self.back_ps).then_inc(V.sem, 1)
            V.wait(dve, s, v + 3)
            scans(self.run, keep, x, self.carried, op0, op1)
            V.wait(dve, s, v + 4)
            nc.vector.tensor_tensor(self.at_end[:], self.run[:], along(ends, HEADS), ALU.mult).then_inc(V.sem, 1)
            V.wait(dve, s, v + 5)
            scans(self.whole, stays, self.at_end, 0.0, ALU.mult, ALU.add, back=True)
            T.wait(dve, s, t + 3)
            nc.vector.tensor_copy(level_back[:, ROWS:], level[:, ROWS:]).then_inc(V.sem, 1)
            V.wait(dve, s, v + 7)
            nc.vector.tensor_tensor_scan(out=level_back[:, 0:ROWS][:, ::-1], data0=row_stays[:, ::-1],
                                         data1=self.level_ps[:, ::-1], initial=level_back[:, ROWS:],
                                         op0=ALU.mult, op1=ALU.add).then_inc(V.sem, 1)
            T.wait(dve, s, t + 4)
            nc.vector.tensor_copy(self.carried[:], self.back_ps).then_inc(V.sem, 1)
            V.wait(dve, s, v + 9)
            scans(self.whole, stays, self.at_end, self.carried, ALU.mult, ALU.add, back=True)

        nc.vector.tensor_copy(self.stays[:], k.stays[:, bass.ds(s, 1), :].rearrange("p a e -> p (a e)")
                              ).then_inc(self.copied, 1)
        nc.vector.tensor_copy(self.row_stays[:], k.row_stays[:, bass.ds(s, 1), :].rearrange("p a e -> p (a e)")
                              ).then_inc(self.copied, 1)
        dve.wait_ge(self.copied, s * 2 + 2)
        stays, row_stays = self.stays[:], self.row_stays[:]
        nc.vector.tensor_copy(self.row_max[:, 0:1], self.row_max[:, ROWS:]).then_inc(V.sem, 1)
        A.wait(dve, s, 1)
        both_ways(self.lg, self.row_max, self.row_max_back, reset, row_reset, -BIG, ALU.add, ALU.max, 1, 1)
        nc.vector.tensor_tensor(self.shift[:], self.row_max[:, 0:1], self.row_max_back[:, 0:1],
                                ALU.subtract).then_inc(V.sem, 1)
        V.wait(dve, s, 12)
        nc.vector.tensor_scalar(self.shift[:], self.shift[:], 0.0, None, ALU.min).then_inc(V.sem, 1)
        nc.vector.tensor_tensor(self.lg[:], self.lg[:], self.whole[:], ALU.subtract).then_inc(V.sem, 1)
        A.wait(dve, s, 3)
        nc.vector.tensor_tensor(self.row_sum[:, 0:1], self.row_sum[:, ROWS:], self.factor[:],
                                ALU.mult).then_inc(V.sem, 1)
        both_ways(self.lg, self.row_sum, self.row_sum_back, goes_on, row_goes_on, 0.0, ALU.mult, ALU.add, 15, 5)
        V.wait(dve, s, 25)
        nc.vector.tensor_scalar(self.whole[:], self.whole[:], 1e-16, None, ALU.max).then_inc(V.sem, 1)
        nc.vector.tensor_scalar(self.factor[:], self.row_sum_back[:, 0:1], 1e-16, None, ALU.max
                                ).then_inc(V.sem, 1)
        V.wait(dve, s, 27)
        nc.vector.reciprocal(self.whole[:], self.whole[:]).then_inc(V.sem, 1)
        nc.vector.reciprocal(self.factor[:], self.factor[:]).then_inc(V.sem, 1)
        V.wait(dve, s, 29)
        nc.vector.tensor_tensor(self.lg[:], self.lg[:], self.whole[:], ALU.mult).then_inc(V.sem, 1)
        nc.vector.tensor_tensor(self.factor[:], self.factor[:], self.row_sum[:, 0:1], ALU.mult
                                ).then_inc(V.sem, 1)
        T.wait(dve, s, 10)
        nc.vector.tensor_copy(self.weights[:], self.weights_ps).then_inc(V.sem, 1)
        nc.vector.tensor_copy(self.rescale[:], self.rescale_ps).then_inc(V.sem, 1)
        V.wait(dve, s, 33)

    def tensor(self, pe, s):
        nc, k, V, T, A = self.nc, self.k, self.V, self.T, self.A
        V.wait_before(pe, s, self.VECTOR_STEPS)
        for h in range(HEADS):
            mm = nc.tensor.transpose(self.rows_ps[:, h, :], self.logits[:, :, h], k.ident[:])
        mm.then_inc(T.sem, 1)

        def both_ways(level, level_back, v):
            V.wait(pe, s, v + 1)
            nc.tensor.transpose(self.level_ps, self.run[:, :, P - 1], k.ident[0:ROWS, 0:ROWS]).then_inc(T.sem, 1)
            V.wait(pe, s, v + 2)
            self.core.hold(pe)
            nc.tensor.transpose(self.back_ps, level[:, 0:ROWS], k.ident[0:HEADS, 0:HEADS]).then_inc(T.sem, 1)
            V.wait(pe, s, v + 6)
            nc.tensor.transpose(self.level_ps, self.whole[:, :, 0], k.ident[0:ROWS, 0:ROWS]).then_inc(T.sem, 1)
            V.wait(pe, s, v + 8)
            self.core.hold(pe)
            nc.tensor.transpose(self.back_ps, level_back[:, 1:ROWS + 1], k.ident[0:HEADS, 0:HEADS]
                                ).then_inc(T.sem, 1)

        both_ways(self.row_max, self.row_max_back, 1)
        both_ways(self.row_sum, self.row_sum_back, 15)
        V.wait(pe, s, 31)
        nc.tensor.matmul(self.rescale_ps, k.heads_on[:], self.factor[:], start=True, stop=True)
        for h in range(HEADS):
            mm = nc.tensor.transpose(self.weights_ps[:, h, :], self.lg[:, h, :], k.ident[0:ROWS, 0:ROWS])
        mm.then_inc(T.sem, 1)

    def scalar(self, act, s):
        nc, V, T, A = self.nc, self.V, self.T, self.A
        T.wait(act, s, 1)
        nc.scalar.activation(self.lg[:], self.rows_ps, ACT.Copy, scale=self.scale).then_inc(A.sem, 1)
        V.wait(act, s, 13)
        nc.scalar.activation(self.factor[:], self.shift[:], ACT.Exp).then_inc(A.sem, 1)
        V.wait(act, s, 14)
        nc.scalar.activation(self.lg[:], self.lg[:], ACT.Exp).then_inc(A.sem, 1)


def attend(core, k, name, table, width, dst_table, dst_width, acc, scale, edge_attr_t=None, w_edge=None):
    nc = core.nc
    edges = edge_attr_t is not None
    ring = RING if edges else LONG_RING
    rounds = GROUPS // ring
    parts = acc.shape[1]
    LOOK = 4 if edges else 2
    with ExitStack() as ctx:
        def sb(n, shape, dt=F32):
            return core.sb(ctx, f"{name}_{n}", shape, dt)

        softmax = SegmentSoftmax(core, k, ctx, name, scale)
        rows = sb("rows", [P, ring, GROUP, width])
        kept = sb("kept", [P, ROWS, D])
        index = sb("index", [P, ring * GROUP], I32)
        target = sb("target", [P, 2, 2, HALF, dst_width])
        local_all = sb("local_all", [P, 2, 2, HALF * P], BF16)
        distance = sb("distance", [P, HALF * P])
        pick = sb("pick", [P, 2, 2, HALF, P])
        hot = sb("hot", [P, 2, HALF, P])
        message = sb("message", [P, 2, HALF, D])
        key = sb("key", [P, 2, HALF, D if edges else HEADS])
        attr = sb("attr", [EDGE_DIM, 2, 2, HALF * P]) if edges else None
        we = sb("we", [EDGE_DIM, D]) if edges else None
        sums = [core.ps(ctx, f"{name}_sums{h}", [P, 1, HALF, P]) for h in range(2)]
        seen = [core.ps(ctx, f"{name}_seen{h}", [P, HALF, D]) for h in range(2)]
        edge_ps = [core.ps(ctx, f"{name}_edge{h}", [P, HALF, D]) for h in range(2)] if edges else None

        staged = core.sem(f"{name}_staged")
        landing = [core.sem(f"{name}_landing{r}") for r in range(ring)]
        landed = core.sem(f"{name}_landed")
        windows = [[core.sem(f"{name}_windows{w}{h}") for h in range(2)] for w in range(2)]
        we_loaded = core.sem(f"{name}_we_loaded")
        distance_ready = core.sem(f"{name}_distance")
        picked = core.sem(f"{name}_pick")
        values_kept = core.sem(f"{name}_values_kept")
        looked = core.sem(f"{name}_looked")
        logit = core.sem(f"{name}_logit_steps")
        weighted = core.sem(f"{name}_weighted")
        spread = core.sem(f"{name}_hot_distance")
        hot_ready = [core.sem(f"{name}_hot_ready{h}") for h in range(2)]
        summed = core.sem(f"{name}_summed")
        added = core.sem(f"{name}_added")
        rescaled = core.sem(f"{name}_rescaled")
        EMPTY = 2 * HALF
        DMAS = HALF + (2 if edges else 1)
        PAIRS = (SUPER_GROUPS - 1) // 2

        block = ctx.enter_context(nc.Block())

        def over_groups(eng, s, group):
            def at(g, w, n):
                G = eng.snap(s * SUPER_GROUPS + g, min_val=0, max_val=GROUPS + SUPER_GROUPS - 1)
                group(G, g, w, n)

            at(0, 1, s * (PAIRS + 1))
            with eng.Fori(0, PAIRS) as pair:
                at(pair * 2 + 1, 0, s * PAIRS + pair)
                at(pair * 2 + 2, 1, s * (PAIRS + 1) + (pair + 1))

        def over_supers(eng, superchunk):
            superchunk(0, True, False)
            with eng.Fori(1, SUPERS) as s:
                superchunk(s, True, True)
            superchunk(SUPERS, False, True)

        @block.gpsimd
        def _(pool):
            def gather(i):
                for r in range(ring):
                    pool.wait_ge(staged, i * ring + (r + 1))
                    core.hold(pool)
                    for c in range(GROUP):
                        nc.gpsimd.indirect_dma_start(
                            out=rows[:, r, c, :], out_offset=None, in_=table,
                            in_offset=bass.IndirectOffsetOnAxis(ap=index[:, r * GROUP + c:r * GROUP + c + 1],
                                                                axis=0)).then_inc(landing[r], 16)
                    if r > 0:
                        pool.wait_ge(landing[r - 1], i * 16 * GROUP + 16 * GROUP)
                        pool.sem_inc(landed, 1)
                    elif not isinstance(i, int):
                        pool.wait_ge(landing[ring - 1], i * 16 * GROUP)
                        pool.sem_inc(landed, 1)

            gather(0)
            with pool.Fori(1, rounds) as i:
                gather(i)
            pool.wait_ge(landing[ring - 1], rounds * 16 * GROUP)
            pool.sem_inc(landed, 1)

        @block.sync
        def _(sp):
            base = [sp.alloc_register(f"{name}_sp_base{c}") for c in range(GROUP)]
            if edges:
                sp.dma_start(we[:], w_edge).then_inc(we_loaded, 16)

            def load_windows(G, g, w, n):
                first_node = load_bases(sp, base, k.base_row, G * GROUP)
                for h in range(2):
                    sp.wait_ge(looked, G * 2 + (h + 3 if isinstance(g, int) else h + 1))
                    local = k.local_rows[bass.ds(G * GROUP + HALF * h, HALF), :]
                    sp.dma_start(local_all[:, w, h, :], local.rearrange("(a c) e -> a (c e)", a=1)
                                 .to_broadcast([P, HALF * P])).then_inc(windows[w][h], 16)
                    if edges:
                        sp.dma_start(attr[:, w, h, :],
                                     edge_attr_t[:, bass.ds(G * (GROUP * P) + HALF * h * P, HALF * P)]
                                     ).then_inc(windows[w][h], 16)
                    for c in range(HALF):
                        sp.dma_start(target[:, w, h, c, :],
                                     dst_table[bass.ds(first_node[HALF * h + c], P), :]).then_inc(windows[w][h], 16)

            with sp.Fori(0, SUPERS) as s:
                over_groups(sp, s, load_windows)

        @block.scalar
        def _(act):
            act.sem_inc(values_kept, 1)

            def stage(group, slot):
                nc.scalar.copy(index[:, bass.ds(slot * GROUP, GROUP)], k.src[:, bass.ds(group * GROUP, GROUP)]
                               ).then_inc(staged, 1)

            for g in range(ring - 1):
                stage(g, g)

            def make_pick(G, w, n, h):
                act.wait_ge(windows[w][h], n * (16 * DMAS) + 16 * DMAS)
                act.wait_ge(picked, G * 2 + (h + 1))
                nc.scalar.activation(distance[:], local_all[:, w, h, :], ACT.Abs, bias=k.iota_p[:], scale=-1.0
                                     ).then_inc(distance_ready, 1)
                act.wait_ge(distance_ready, G * 2 + (h + 1))
                nc.scalar.activation(pick[:, w, h, :, :].rearrange("p c e -> p (c e)"), distance[:],
                                     ACT.Relu, bias=1.0, scale=-1.0).then_inc(picked, 1)

            def make_hot(B, h):
                act.wait_ge(summed, B * 2 + (h + 1))
                for c in range(HALF):
                    mark = nc.scalar.activation(hot[:, h, c, :], k.iota[:], ACT.Abs, scale=-1.0,
                                                bias=k.local[:, bass.ds(B * GROUP + (HALF * h + c), 1)])
                mark.then_inc(spread, 1)
                act.wait_ge(spread, B * (2 if edges else 1) + (h + 1))
                half = hot[:, h, :, :].rearrange("p c n -> p (c n)")
                nc.scalar.activation(half, half, ACT.Relu, bias=1.0, scale=-1.0).then_inc(hot_ready[h], 1)

            def superchunk(s, gathered, summing):
                def group(G, g, w, n):
                    if gathered:
                        for h in range(2):
                            act.wait_ge(looked, G * 2 + (h + 3 if isinstance(g, int) else h + 1))
                            make_pick(G, w, n, h)
                        act.wait_ge(logit, G * (2 * LOOK) + 2 * LOOK)
                        if not edges:
                            act.wait_ge(values_kept, G + 1)
                        stage(G + (ring - 1), act.snap((G + (ring - 1)) & (ring - 1), min_val=0, max_val=ring - 1))
                    if summing:
                        B = act.snap(G - SUPER_GROUPS, min_val=0, max_val=GROUPS - 1)
                        for h in range(2 if edges else 1):
                            make_hot(B, h)
                    if gathered and not edges:
                        act.wait_ge(landed, G + 1)
                        slot = act.snap(G & (ring - 1), min_val=0, max_val=ring - 1)
                        if summing:
                            act.wait_ge(weighted, B * 2 + 2)
                        nc.scalar.copy(kept[:, bass.ds(g * GROUP, GROUP), :],
                                       rows[:, bass.ds(slot, 1), :, 0:D].rearrange("p a c f -> p (a c) f")
                                       ).then_inc(values_kept, 1)

                over_groups(act, s, group)
                if gathered:
                    softmax.scalar(act, s)

            act.sem_inc(picked, 1)
            softmax.A.start(act)
            over_supers(act, superchunk)

        @block.tensor
        def _(pe):
            pe.sem_inc(looked, 4)
            pe.sem_inc(summed, 2)
            softmax.T.start(pe)
            if edges:
                pe.wait_ge(we_loaded, 16)

            def look(G, w, n, h):
                pe.wait_ge(windows[w][h], n * (16 * DMAS) + 16 * DMAS)
                pe.wait_ge(picked, G * 2 + (h + 2))
                pe.wait_ge(logit, G * (2 * LOOK) + (h + 1) * LOOK)
                for c in range(HALF):
                    mm = nc.tensor.matmul(seen[h][:, c, 0:dst_width], pick[:, w, h, c, :],
                                          target[:, w, h, c, :], start=True, stop=True)
                    if edges:
                        mm = nc.tensor.matmul(edge_ps[h][:, c, :], attr[:, w, h, c * P:(c + 1) * P], we[:],
                                              start=True, stop=True)
                mm.then_inc(looked, 1)

            def sum_up(B, h):
                pe.wait_ge(hot_ready[h], B + 1)
                pe.wait_ge(weighted, B * 2 + (h + 1))
                pe.wait_ge(added, B * (2 * HALF) + (HALF * h + HALF))
                for c in range(HALF):
                    mm = nc.tensor.matmul(sums[h][:, 0, c, :], message[:, h, c, :], hot[:, h, c, :],
                                          start=True, stop=True)
                mm.then_inc(summed, 1)

            def superchunk(s, gathered, summing):
                def group(G, g, w, n):
                    if gathered:
                        for h in range(2):
                            look(G, w, n, h)
                    if summing:
                        B = pe.snap(G - SUPER_GROUPS, min_val=0, max_val=GROUPS - 1)
                        for h in range(2):
                            sum_up(B, h)

                over_groups(pe, s, group)
                if gathered:
                    pe.wait_ge(logit, s * (SUPER_GROUPS * 2 * LOOK) + (SUPER_GROUPS * 2 + 2) * LOOK)
                    softmax.tensor(pe, s)

            over_supers(pe, superchunk)

        @block.vector
        def _(dve):
            base = [dve.alloc_register(f"{name}_base{c}") for c in range(GROUP)]
            nc.vector.memset(acc, 0.0).then_inc(added, EMPTY)
            dve.sem_inc(logit, 2 * LOOK)
            softmax.start_vector(dve)

            def weigh(B, g, h):
                dve.wait_ge(summed, B * 2 + (h + 1))
                weight = softmax.weights[:, :, bass.ds(g * GROUP + HALF * h, HALF)].rearrange("p h j -> p j h")
                nc.vector.tensor_tensor(message[:, h, :, :].rearrange("p j (h c) -> p j h c", h=HEADS),
                                        kept[:, bass.ds(g * GROUP + HALF * h, HALF), :]
                                        .rearrange("p j (h c) -> p j h c", h=HEADS),
                                        weight.unsqueeze(3).to_broadcast([P, HALF, HEADS, HC]),
                                        ALU.mult).then_inc(weighted, 1)

            def look(G, g, h, slot, summing, step):
                row = rows[:, bass.ds(slot, 1), HALF * h:HALF * (h + 1), :].rearrange("p a c f -> p (a c) f")
                logits = softmax.logits[:, bass.ds(g * GROUP + HALF * h, HALF), :]
                done = G * (2 * LOOK) + (2 + h) * LOOK
                if step == 1:
                    if h == 0:
                        dve.wait_ge(landed, G + 1)
                    dve.wait_ge(looked, G * 2 + (h + 5))
                if not edges:
                    if step == 1:
                        nc.vector.tensor_tensor(key[:, h, :, :], row[:, :, D:D + HEADS], seen[h][:, :, 0:HEADS],
                                                ALU.add).then_inc(logit, 1)
                    else:
                        dve.wait_ge(logit, done + 1)
                        nc.vector.scalar_tensor_tensor(out=logits, in0=key[:, h, :, :], scalar=0.2,
                                                       in1=key[:, h, :, :], op0=ALU.mult, op1=ALU.max
                                                       ).then_inc(logit, 1)
                elif step == 1:
                    nc.vector.tensor_tensor(key[:, h, :, :], row[:, :, 0:D], edge_ps[h][:], ALU.add
                                            ).then_inc(logit, 1)
                elif step == 2:
                    if summing:
                        dve.wait_ge(weighted, (G - SUPER_GROUPS) * 2 + (h + 1))
                    nc.vector.tensor_tensor(kept[:, bass.ds(g * GROUP + HALF * h, HALF), :], row[:, :, D:2 * D],
                                            edge_ps[h][:], ALU.add).then_inc(logit, 1)
                elif step == 3:
                    dve.wait_ge(logit, done + 1)
                    nc.vector.tensor_tensor(key[:, h, :, :], key[:, h, :, :], seen[h][:], ALU.mult
                                            ).then_inc(logit, 1)
                else:
                    dve.wait_ge(logit, done + 3)
                    nc.vector.tensor_reduce(logits, key[:, h, :, :].rearrange("p j (h c) -> p j h c", h=HEADS),
                                            AX_X, ALU.add).then_inc(logit, 1)

            def make_hot(B):
                nc.vector.tensor_tensor(hot[:, 1, :, :], wide(k.local[:, bass.ds(B * GROUP + HALF, HALF)], P),
                                        along(k.iota[:], HALF), ALU.is_equal).then_inc(hot_ready[1], 1)

            def add(B, h, c, first_node):
                if c == 0:
                    dve.wait_ge(summed, B * 2 + (h + 3))
                dve.wait_ge(added, B * (2 * HALF) + (EMPTY + HALF * h + c + 1 - parts))
                window = acc[:, c % parts, bass.ds(first_node[HALF * h + c], P)]
                nc.vector.tensor_tensor(window, window, sums[h][:, 0, c, :], ALU.add).then_inc(added, 1)

            def superchunk(s, gathered, summing):
                def group(G, g, w, n):
                    if gathered:
                        slot = dve.snap(G & (ring - 1), min_val=0, max_val=ring - 1)
                        look_step = lambda h, step: look(G, g, h, slot, summing, step)
                    else:
                        look_step = lambda h, step: None
                    if not summing:
                        for h in range(2):
                            for step in range(1, LOOK + 1):
                                look_step(h, step)
                        return
                    B = dve.snap(G - SUPER_GROUPS, min_val=0, max_val=GROUPS - 1)
                    weigh(B, g, 0)
                    weigh(B, g, 1)
                    if edges:
                        look_step(0, 1)
                        look_step(0, 2)
                    first_node = load_bases(dve, base, k.base_row, B * GROUP)
                    if edges:
                        look_step(0, 3)
                        between = [(0, 4), (1, 1), (1, 2), (1, 3), (1, 4)]
                    else:
                        look_step(0, 1)
                        look_step(0, 2)
                        between = [(1, 1), (1, 2)]
                    for n in range(GROUP):
                        add(B, n // HALF, n % HALF, first_node)
                        if n < len(between):
                            look_step(*between[n])
                        elif not edges and n == HALF:
                            make_hot(B + 1)

                over_groups(dve, s, group)
                if gathered:
                    softmax.vector(dve, s)
                    dve.load([base[0]], k.base_row[0:1, bass.ds(s * ROWS, 1)])
                    node = dve.snap(base[0], min_val=0, max_val=N_NODES)
                    if summing:
                        dve.wait_ge(added, s * ROWS + EMPTY)
                    else:
                        dve.wait_ge(added, EMPTY)
                    column = acc[:, :, bass.ds(node, 1)]
                    nc.vector.tensor_scalar(column, column, softmax.rescale[:], None, ALU.mult
                                            ).then_inc(rescaled, 1)
                    dve.wait_ge(rescaled, s + 1)

            if not edges:
                make_hot(0)
            over_supers(dve, superchunk)
            dve.wait_ge(added, EMPTY + CHUNKS)
            if parts == 2:
                nc.vector.tensor_tensor(acc[:, 0, :], acc[:, 0, :], acc[:, 1, :], ALU.add).then_inc(added, 1)


def leave_l1(core, k, ins, acc, x_in, x_out, table):
    nc = core.nc
    with ExitStack() as ctx:
        def sb(name, shape, dt=F32):
            return core.sb(ctx, f"l1n_{name}", shape, dt)

        def of_lanes(name, shape):
            return [sb(f"{name}{lane}", shape) for lane in LANES]

        bias = sb("bias", [P, D])
        features = of_lanes("features", [P, QUAD * P])
        x = of_lanes("x", [P, QUAD, D])
        z = of_lanes("z", [P, QUAD, D])
        weighted = of_lanes("weighted", [P, QUAD, D + 1])
        norm = [Norm(core, ctx, f"l1n_{lane}", z[lane]) for lane in LANES]
        nodes = [core.ps(ctx, f"l1n_nodes{lane}", [P, QUAD, D]) for lane in LANES]
        loaded = core.sem("l1n_loaded")
        x_loaded = [core.sem(f"l1n_x_loaded{lane}") for lane in LANES]
        ready = core.sem("l1n_eps")
        A = [Steps(core, f"l1n_scalar{lane}", 2) for lane in LANES]
        T = [Steps(core, f"l1n_tensor{lane}", 1) for lane in LANES]
        V = [Steps(core, f"l1n_vector{lane}", 8) for lane in LANES]
        stored = [Steps(core, f"l1n_stored{lane}", 32) for lane in LANES]
        STAGES = 8
        block = ctx.enter_context(nc.Block())

        @block.gpsimd
        def _(pool):
            def load_x(i, n, lane):
                V[lane].wait_before(pool, n, 1)
                pool.dma_start(x[lane][:], rows_of(x_in, i)).then_inc(x_loaded[lane], 16)

            in_lanes(pool, STAGES, {0: load_x})

        @block.sync
        def _(sp):
            sp.dma_start(bias[:], ins["L1_gnn_bias"].rearrange("(a f) -> a f", a=1).to_broadcast([P, D])
                         ).then_inc(loaded, 16)

            def store(i, n, lane):
                V[lane].wait(sp, n, 8)
                sp.dma_start(rows_of(x_out, i), z[lane][:]).then_inc(stored[lane].sem, 16)
                sp.dma_start(rows_of(table, i), weighted[lane][:]).then_inc(stored[lane].sem, 16)

            for lane in LANES:
                stored[lane].start(sp)
            in_lanes(sp, STAGES, {STAGES - 1: store})
            for lane in LANES:
                stored[lane].wait_before(sp, (QUADS + 1 - lane) // 2, 32)

        @block.vector
        def _(dve):
            for lane in LANES:
                V[lane].start(dve)
                nc.vector.memset(norm[lane].eps[:], EPS).then_inc(ready, 1)
            dve.wait_ge(loaded, 16)

            def add_x(i, n, lane):
                T[lane].wait(dve, n, 1)
                dve.wait_ge(x_loaded[lane], n * 16 + 16)
                stored[lane].wait_before(dve, n, 32)
                nc.vector.tensor_tensor(z[lane][:], nodes[lane][:], x[lane][:], ALU.add).then_inc(V[lane].sem, 1)

            def center(i, n, lane):
                V[lane].wait(dve, n, 1)
                nc.vector.tensor_tensor(z[lane][:], z[lane][:], along(bias[:], QUAD), ALU.add
                                        ).then_inc(V[lane].sem, 1)
                norm[lane].take_statistics(dve, n, V[lane], 2)

            def rescale(i, n, lane):
                norm[lane].rescale(dve, n, V[lane], 2, A[lane], 2)

            def weigh(i, n, lane):
                V[lane].wait(dve, n, 6)
                inverse = k.deg_inv[:, bass.ds(i * QUAD, QUAD)]
                nc.vector.tensor_tensor(weighted[lane][:, :, 0:D], z[lane][:], wide(inverse, D), ALU.mult
                                        ).then_inc(V[lane].sem, 1)
                nc.vector.tensor_copy(weighted[lane][:, :, D:D + 1], wide(inverse, 1)).then_inc(V[lane].sem, 1)

            in_lanes(dve, STAGES, {2: add_x, 3: center, 5: rescale, 6: weigh})

        @block.tensor
        def _(pe):
            def to_nodes(i, n, lane):
                A[lane].wait(pe, n, 1)
                V[lane].wait_before(pe, n, 1)
                for t in range(QUAD):
                    mm = nc.tensor.transpose(nodes[lane][:, t, :], features[lane][:, t * P:(t + 1) * P], k.ident[:])
                mm.then_inc(T[lane].sem, 1)

            for lane in LANES:
                T[lane].start(pe)
            in_lanes(pe, STAGES, {1: to_nodes})

        @block.scalar
        def _(act):
            def fetch(i, n, lane):
                T[lane].wait_before(act, n, 1)
                nc.scalar.copy(features[lane][:], acc[:, 0, bass.ds(i * (QUAD * P), QUAD * P)]
                               ).then_inc(A[lane].sem, 1)

            def root(i, n, lane):
                norm[lane].root(act, n, V[lane], 2, A[lane])

            for lane in LANES:
                A[lane].start(act)
            act.wait_ge(ready, 2)
            in_lanes(act, STAGES, {0: fetch, 4: root})


def leave_l2(core, k, ins, acc, x_in, table, dst_table, x_skip):
    nc = core.nc
    with ExitStack() as ctx:
        def sb(name, shape, dt=F32):
            return core.sb(ctx, f"l2_{name}", shape, dt)

        def of_lanes(name, shape):
            return [sb(f"{name}{lane}", shape) for lane in LANES]

        def ps_of_lanes(name, shape):
            return [core.ps(ctx, f"l2_{name}{lane}", shape) for lane in LANES]

        w3t = sb("w3t", [P, D])
        bias = sb("bias", [P, D])
        w_all = sb("w_all", [P, 4 * D])
        b_all = sb("b_all", [P, 4 * D])
        features = of_lanes("features", [P, QUAD * P])
        counts = of_lanes("counts", [1, QUAD * P])
        x = of_lanes("x", [P, QUAD, D])
        cross = of_lanes("cross", [P, QUAD, D])
        cross_t = of_lanes("cross_t", [P, QUAD * P])
        z = of_lanes("z", [P, QUAD, D])
        z_t = of_lanes("z_t", [P, QUAD * P])
        n_sum = of_lanes("n_sum", [P, QUAD])
        heads = of_lanes("heads", [P, QUAD, 4 * D])
        norm = [Norm(core, ctx, f"l2_{lane}", z[lane]) for lane in LANES]
        nodes = ps_of_lanes("nodes", [P, QUAD, D])
        out_ps = nodes
        turned_ps = ps_of_lanes("turned", [P, QUAD, D])
        heads_ps = ps_of_lanes("heads_ps", [P, QUAD // 2, 4 * D])
        n_ps = [ps[:, 0, 0:QUAD] for ps in heads_ps]
        loaded = core.sem("l2_loaded")
        x_loaded = [core.sem(f"l2_x_loaded{lane}") for lane in LANES]
        ready = core.sem("l2_ready")
        A = [Steps(core, f"l2_scalar{lane}", 5) for lane in LANES]
        T = [Steps(core, f"l2_tensor{lane}", 6) for lane in LANES]
        V = [Steps(core, f"l2_vector{lane}", 14) for lane in LANES]
        stored = [Steps(core, f"l2_stored{lane}", 64) for lane in LANES]
        STAGES = 16
        block = ctx.enter_context(nc.Block())

        @block.gpsimd
        def _(pool):
            def load_x(i, n, lane):
                V[lane].wait_before(pool, n, 8)
                pool.dma_start(x[lane][:], rows_of(x_in, i)).then_inc(x_loaded[lane], 16)

            in_lanes(pool, STAGES, {0: load_x})

        @block.sync
        def _(sp):
            sp.dma_start(w3t[:], ins["w3_t"]).then_inc(loaded, 16)
            sp.dma_start(bias[:], ins["L2_gnn_W1_b"].rearrange("(a f) -> a f", a=1).to_broadcast([P, D])
                         ).then_inc(loaded, 16)
            for n, part in enumerate(("k", "v", "q", "skip")):
                sp.dma_start(w_all[:, n * D:(n + 1) * D], ins[f"L3_gnn_W{part}"]).then_inc(loaded, 16)
                sp.dma_start(b_all[:, n * D:(n + 1) * D], ins[f"L3_gnn_b{part}"].rearrange("(a f) -> a f", a=1)
                             .to_broadcast([P, D])).then_inc(loaded, 16)

            def store_x(i, n, lane):
                V[lane].wait(sp, n, 12)
                sp.dma_start(rows_of(x_skip[:, 0:D], i), z[lane][:]).then_inc(stored[lane].sem, 16)

            def store_heads(i, n, lane):
                V[lane].wait(sp, n, 14)
                sp.dma_start(rows_of(table, i), heads[lane][:, :, 0:2 * D]).then_inc(stored[lane].sem, 16)
                sp.dma_start(rows_of(dst_table, i), heads[lane][:, :, 2 * D:3 * D]).then_inc(stored[lane].sem, 16)
                sp.dma_start(rows_of(x_skip[:, D:2 * D], i), heads[lane][:, :, 3 * D:]
                             ).then_inc(stored[lane].sem, 16)

            for lane in LANES:
                stored[lane].start(sp)
            in_lanes(sp, STAGES, {9: store_x, 15: store_heads})
            for lane in LANES:
                stored[lane].wait_before(sp, (QUADS + 1 - lane) // 2, 64)

        @block.vector
        def _(dve):
            for lane in LANES:
                V[lane].start(dve)
                nc.vector.memset(norm[lane].eps[:], EPS).then_inc(ready, 1)
            dve.wait_ge(loaded, 160)

            def cross_terms(i, n, lane):
                T[lane].wait(dve, n, 1)
                dve.wait_ge(x_loaded[lane], n * 16 + 16)
                nc.vector.tensor_tensor(cross[lane][:], nodes[lane][:], x[lane][:], ALU.mult
                                        ).then_inc(V[lane].sem, 1)
                nc.vector.tensor_copy(n_sum[lane][:], n_ps[lane]).then_inc(V[lane].sem, 1)
                stored[lane].wait_before(dve, n, 64)
                nc.vector.tensor_tensor(z[lane][:], x[lane][:], along(bias[:], QUAD), ALU.add
                                        ).then_inc(V[lane].sem, 1)
                V[lane].wait(dve, n, 3)
                nc.vector.tensor_tensor(z[lane][:], z[lane][:], wide(n_sum[lane][:], D), ALU.mult
                                        ).then_inc(V[lane].sem, 1)

            def add_up(i, n, lane):
                zl = z[lane][:]
                V[lane].wait(dve, n, 4)
                T[lane].wait(dve, n, 3)
                nc.vector.tensor_tensor(zl, zl, out_ps[lane][:], ALU.add).then_inc(V[lane].sem, 1)
                V[lane].wait(dve, n, 5)
                nc.vector.tensor_tensor(zl, zl, wide(k.deg_inv[:, bass.ds(i * QUAD, QUAD)], D), ALU.mult
                                        ).then_inc(V[lane].sem, 1)
                V[lane].wait(dve, n, 6)
                nc.vector.scalar_tensor_tensor(out=zl, in0=zl, scalar=0.01, in1=zl, op0=ALU.mult, op1=ALU.max
                                               ).then_inc(V[lane].sem, 1)
                V[lane].wait(dve, n, 7)
                nc.vector.tensor_tensor(zl, zl, x[lane][:], ALU.add).then_inc(V[lane].sem, 1)
                norm[lane].take_statistics(dve, n, V[lane], 8)

            def rescale(i, n, lane):
                norm[lane].rescale(dve, n, V[lane], 8, A[lane], 4)

            def take_heads(half):
                def take(i, n, lane):
                    T[lane].wait(dve, n, 5 + half)
                    nc.vector.tensor_tensor(heads[lane][:, 2 * half:2 * half + 2, :], heads_ps[lane][:],
                                            along(b_all[:], 2), ALU.add).then_inc(V[lane].sem, 1)
                return take

            in_lanes(dve, STAGES, {2: cross_terms, 6: add_up, 8: rescale, 12: take_heads(0), 14: take_heads(1)})

        @block.tensor
        def _(pe):
            pe.wait_ge(loaded, 160)

            def to_nodes(i, n, lane):
                A[lane].wait(pe, n, 2)
                V[lane].wait_before(pe, n, 14)
                for t in range(QUAD):
                    nc.tensor.transpose(nodes[lane][:, t, :], features[lane][:, t * P:(t + 1) * P], k.ident[:])
                for t in range(QUAD):
                    mm = nc.tensor.transpose(n_ps[lane][:, t:t + 1], counts[lane][:, t * P:(t + 1) * P],
                                             k.ident[0:1, 0:1])
                mm.then_inc(T[lane].sem, 1)

            def turn_cross(i, n, lane):
                V[lane].wait(pe, n, 1)
                for t in range(QUAD):
                    mm = nc.tensor.transpose(turned_ps[lane][:, t, :], cross[lane][:, t, :], k.ident[:])
                mm.then_inc(T[lane].sem, 1)

            def linear(i, n, lane):
                A[lane].wait(pe, n, 3)
                for t in range(QUAD):
                    mm = nc.tensor.matmul(out_ps[lane][:, t, :], cross_t[lane][:, t * P:(t + 1) * P], w3t[:],
                                          start=True, stop=True)
                mm.then_inc(T[lane].sem, 1)

            def turn_x(i, n, lane):
                V[lane].wait(pe, n, 12)
                for t in range(QUAD):
                    mm = nc.tensor.transpose(turned_ps[lane][:, t, :], z[lane][:, t, :], k.ident[:])
                mm.then_inc(T[lane].sem, 1)

            def project(half):
                def part(i, n, lane):
                    if half == 0:
                        A[lane].wait(pe, n, 5)
                    else:
                        V[lane].wait(pe, n, 13)
                    for t in range(2):
                        node = (2 * half + t) * P
                        mm = nc.tensor.matmul(heads_ps[lane][:, t, :], z_t[lane][:, node:node + P], w_all[:],
                                              start=True, stop=True)
                    mm.then_inc(T[lane].sem, 1)
                return part

            for lane in LANES:
                T[lane].start(pe)
            in_lanes(pe, STAGES, {1: to_nodes, 3: turn_cross, 5: linear, 9: turn_x, 11: project(0), 13: project(1)})

        @block.scalar
        def _(act):
            def fetch(i, n, lane):
                T[lane].wait_before(act, n, 1)
                nc.scalar.copy(features[lane][:], acc[:, 0, bass.ds(i * (QUAD * P), QUAD * P)]
                               ).then_inc(A[lane].sem, 1)
                nc.scalar.copy(counts[lane][:], acc[0:1, 1, bass.ds(i * (QUAD * P), QUAD * P)]
                               ).then_inc(A[lane].sem, 1)

            def take_cross(i, n, lane):
                T[lane].wait(act, n, 2)
                nc.scalar.copy(cross_t[lane][:].rearrange("p (t n) -> p t n", t=QUAD), turned_ps[lane][:]
                               ).then_inc(A[lane].sem, 1)

            def root(i, n, lane):
                norm[lane].root(act, n, V[lane], 8, A[lane])

            def take_x(i, n, lane):
                T[lane].wait(act, n, 4)
                nc.scalar.copy(z_t[lane][:].rearrange("p (t n) -> p t n", t=QUAD), turned_ps[lane][:]
                               ).then_inc(A[lane].sem, 1)

            for lane in LANES:
                A[lane].start(act)
            act.wait_ge(ready, 2)
            in_lanes(act, STAGES, {0: fetch, 4: take_cross, 7: root, 10: take_x})


def leave_l3(core, k, acc, x_skip, out):
    nc = core.nc
    with ExitStack() as ctx:
        def of_lanes(name, shape):
            return [core.sb(ctx, f"l3n_{name}{lane}", shape) for lane in LANES]

        features = of_lanes("features", [P, QUAD * P])
        x = of_lanes("x", [P, QUAD, 2 * D])
        z = of_lanes("z", [P, QUAD, D])
        norm = [Norm(core, ctx, f"l3n_{lane}", z[lane]) for lane in LANES]
        nodes = [core.ps(ctx, f"l3n_nodes{lane}", [P, QUAD, D]) for lane in LANES]
        x_loaded = [core.sem(f"l3n_x_loaded{lane}") for lane in LANES]
        ready = core.sem("l3n_eps")
        A = [Steps(core, f"l3n_scalar{lane}", 2) for lane in LANES]
        T = [Steps(core, f"l3n_tensor{lane}", 1) for lane in LANES]
        V = [Steps(core, f"l3n_vector{lane}", 6) for lane in LANES]
        stored = [Steps(core, f"l3n_stored{lane}", 16) for lane in LANES]
        STAGES = 8
        block = ctx.enter_context(nc.Block())

        @block.gpsimd
        def _(pool):
            def load_x(i, n, lane):
                V[lane].wait_before(pool, n, 2)
                pool.dma_start(x[lane][:], rows_of(x_skip, i)).then_inc(x_loaded[lane], 16)

            in_lanes(pool, STAGES, {0: load_x})

        @block.sync
        def _(sp):
            def store(i, n, lane):
                V[lane].wait(sp, n, 6)
                if isinstance(i, int) and i == QUADS - 1:
                    sp.dma_start(out[FULL_TILES * P:N_NODES, :], z[lane][0:TAIL, 0, :]
                                 ).then_inc(stored[lane].sem, 16)
                else:
                    sp.dma_start(rows_of(out, i), z[lane][:]).then_inc(stored[lane].sem, 16)

            for lane in LANES:
                stored[lane].start(sp)
            in_lanes(sp, STAGES, {STAGES - 1: store})
            for lane in LANES:
                stored[lane].wait_before(sp, (QUADS + 1 - lane) // 2, 16)

        @block.vector
        def _(dve):
            def add_x(i, n, lane):
                zl, xl = z[lane][:], x[lane]
                T[lane].wait(dve, n, 1)
                dve.wait_ge(x_loaded[lane], n * 16 + 16)
                stored[lane].wait_before(dve, n, 16)
                nc.vector.tensor_tensor(zl, nodes[lane][:], xl[:, :, D:2 * D], ALU.add).then_inc(V[lane].sem, 1)

            def center(i, n, lane):
                zl, xl = z[lane][:], x[lane]
                V[lane].wait(dve, n, 1)
                nc.vector.scalar_tensor_tensor(out=zl, in0=zl, scalar=0.0, in1=xl[:, :, 0:D], op0=ALU.max,
                                               op1=ALU.add).then_inc(V[lane].sem, 1)
                norm[lane].take_statistics(dve, n, V[lane], 2)

            def rescale(i, n, lane):
                norm[lane].rescale(dve, n, V[lane], 2, A[lane], 2)

            for lane in LANES:
                V[lane].start(dve)
                nc.vector.memset(norm[lane].eps[:], EPS).then_inc(ready, 1)
            in_lanes(dve, STAGES, {2: add_x, 3: center, 5: rescale})

        @block.tensor
        def _(pe):
            def to_nodes(i, n, lane):
                A[lane].wait(pe, n, 1)
                V[lane].wait_before(pe, n, 1)
                for t in range(QUAD):
                    mm = nc.tensor.transpose(nodes[lane][:, t, :], features[lane][:, t * P:(t + 1) * P], k.ident[:])
                mm.then_inc(T[lane].sem, 1)

            for lane in LANES:
                T[lane].start(pe)
            in_lanes(pe, STAGES, {1: to_nodes})

        @block.scalar
        def _(act):
            def fetch(i, n, lane):
                T[lane].wait_before(act, n, 1)
                nc.scalar.copy(features[lane][:], acc[:, 0, bass.ds(i * (QUAD * P), QUAD * P)]
                               ).then_inc(A[lane].sem, 1)

            def root(i, n, lane):
                norm[lane].root(act, n, V[lane], 2, A[lane])

            for lane in LANES:
                A[lane].start(act)
            act.wait_ge(ready, 2)
            in_lanes(act, STAGES, {0: fetch, 4: root})


def build(nc, ins, out):
    core = Core(nc)
    with ExitStack() as ctx:
        k = Kept(core, ctx)
        with ExitStack() as l0:
            k.x = core.sb(l0, "x_nodes", [P, TILES, D])
            k.scaled = core.sb(l0, "x_scaled", [P, TILES, D])
            acc = core.sb(l0, "l0_acc", [P, 1, N_PAD])
            set_up(core, k, ins["x"], ins["src_cols"], ins["dst_cols"], ins["base_row"])
            scale_nodes(core, k, k.table0)
            sum_over_edges(core, k, "hop1", k.table0, D, acc[:], 1)
            propagate_nodes(core, k, acc, k.table0b)
            sum_over_edges(core, k, "hop2", k.table0b, D, acc[:], 1)
            leave_l0(core, k, ins, acc, k.x1, k.table1, k.dst1)
        mark_segments(core, k, ins["dst_line"])
        with ExitStack() as l1:
            acc = core.sb(l1, "l1_acc", [P, 2, N_PAD])
            attend(core, k, "l1", k.table1, D + HEADS, k.dst1, HEADS, acc[:], 1.0)
            leave_l1(core, k, ins, acc, k.x1, k.x2, k.table2)
        with ExitStack() as l2:
            acc = core.sb(l2, "l2_acc", [P, 2, N_PAD])
            sum_over_edges(core, k, "l2", k.table2, D + 1, acc[:], 2)
            leave_l2(core, k, ins, acc, k.x2, k.table3, k.dst3, k.x_skip)
        with ExitStack() as l3:
            acc = core.sb(l3, "l3_acc", [P, 1, N_PAD])
            attend(core, k, "l3", k.table3, 2 * D, k.dst3, D, acc[:], float(HC) ** -0.5,
                   ins["edge_attr_t"], ins["L3_gnn_We"])
            leave_l3(core, k, acc, k.x_skip, out)


def kernel(**inputs):
    import concourse.bacc as bacc
    from concourse.bass_utils import run_bass_kernel_spmd

    nc = bacc.Bacc("TRN2", target_bir_lowering=False, num_devices=1)
    src = np.asarray(inputs["src"])
    dst = np.asarray(inputs["dst"])
    pad = E_PAD - N_EDGES
    src = np.concatenate([src, np.zeros(pad, src.dtype)])
    dst = np.concatenate([np.full(1, -1, dst.dtype), dst, np.full(pad + 1, N_NODES, dst.dtype)])
    arrays = {name: np.ascontiguousarray(a) for name, a in inputs.items()
              if name not in ("src", "dst", "edge_attr_32", "edge_weight")}
    arrays["src_cols"] = np.ascontiguousarray(src.reshape(CHUNKS, CHUNK).T)
    arrays["dst_cols"] = np.ascontiguousarray(dst[1:-1].reshape(CHUNKS, CHUNK).T)
    arrays["base_row"] = np.ascontiguousarray(dst[1:-1:CHUNK].reshape(1, CHUNKS))
    arrays["dst_line"] = dst
    arrays["w2_t"] = np.ascontiguousarray(arrays.pop("L0_gnn_w2").T)
    arrays["w3_t"] = np.ascontiguousarray(arrays.pop("L2_gnn_W1_w").T)
    edge_attr = np.asarray(inputs["edge_attr_32"])
    arrays["edge_attr_t"] = np.ascontiguousarray(
        np.concatenate([edge_attr, np.zeros((pad, EDGE_DIM), edge_attr.dtype)]).T)
    ins = {name: nc.dram_tensor(f"in_{name}", a.shape, mybir.dt.from_np(a.dtype), kind="ExternalInput").ap()
           for name, a in arrays.items()}
    out = nc.dram_tensor("out", (N_NODES, D), F32, kind="ExternalOutput").ap()
    build(nc, ins, out)
    r = run_bass_kernel_spmd(nc, [{f"in_{name}": a for name, a in arrays.items()}], core_ids=[0])
    return r.results[0]["out"]
```
